# Optimizing a Trainium2 kernel written in Bass

```python
import numpy as np
import jax
import jax.numpy as jnp

def _softmax(x, axis=-1):
    return jax.nn.softmax(x, axis=axis)

def _gelu(x):
    return jax.nn.gelu(x, approximate=True)

def _silu(x):
    return jax.nn.silu(x)

def _sigmoid(x):
    return jax.nn.sigmoid(x)

def _layernorm(x, axis=-1, eps=1e-05):
    m = jnp.mean(x, axis=axis, keepdims=True)
    v = jnp.var(x, axis=axis, keepdims=True)
    return (x - m) / jnp.sqrt(v + eps)

def _scatter_add(tgt, idx, src, axis=0):
    return tgt.at[idx].add(src)

def _segment_sum(src, seg, n):
    return jax.ops.segment_sum(src, seg, n)
kernel_name = 'mk_adj_resnorm_d4_adj_r2_c964ce'

def setup_inputs(seed: int=0):
    np.random.seed(seed)
    _w = jnp.asarray

    def _rec_inputs():
        import jax
        import jax.numpy as jnp
        _gk = jax.random.key(seed)
        x = -0.0005207 + 1.001 * jax.random.normal(jax.random.fold_in(_gk, 1), (8192, 128), jnp.float32)
        _a = jax.random.bernoulli(jax.random.fold_in(_gk, 2), 0.000488281, (8192, 8192))
        _a = jnp.logical_or(_a, jnp.swapaxes(_a, -1, -2))
        _a = jnp.logical_or(_a, jnp.eye(8192, dtype=bool))
        adj = _a.astype(jnp.int32)
        return (x, adj)
    x, adj = _rec_inputs()

    def _L0_gnn_setup():
        import jax, jax.numpy as jnp
        import numpy as np
        NEG_INF = -9000000000000000.0
        key = jax.random.key(seed)
        k1, k2, k3, k4 = jax.random.split(key, 4)
        N, F = (4096, 128)
        node = jax.random.normal(k1, (N, F), dtype=jnp.float32)
        adj = jax.random.randint(k2, (N, N), 0, 2, dtype=jnp.int32)
        W = jax.random.normal(k3, (F, F), dtype=jnp.float32) * (1.0 / np.sqrt(F))
        a = jax.random.normal(k4, (2 * F, 1), dtype=jnp.float32) * (1.0 / np.sqrt(F))
        return {'node': node, 'adj': adj, 'W': W, 'a': a}
    _L0_gnn_all = _L0_gnn_setup()
    _L0_gnn_in = {k: v for k, v in _L0_gnn_all.items() if k in ('W', 'a')}
    del _L0_gnn_all

    def _L1_gnn_setup():
        import jax, jax.numpy as jnp
        import numpy as np
        N = 2048
        IN_F = 128
        OUT_F = 128
        HEADS = 4
        HEAD_DIM = OUT_F // HEADS
        ALPHA = 0.2
        NEG_INF = -9000000000000000.0
        LN_EPS = 1e-05
        key = jax.random.key(seed)
        k1, k2, k3, k4 = jax.random.split(key, 4)
        x = jax.random.normal(k1, (N, IN_F), dtype=jnp.float32)
        adj = jax.random.randint(k2, (N, N), 0, 2, dtype=jnp.int32)

        def xavier(k, shape, gain=1.414):
            fan_in, fan_out = (shape[0], shape[1])
            bound = gain * np.sqrt(6.0 / (fan_in + fan_out))
            return jax.random.uniform(k, shape, jnp.float32, -bound, bound)
        W = xavier(k3, (IN_F, OUT_F))
        a = xavier(k4, (2 * HEAD_DIM, 1))
        gamma = jnp.ones((OUT_F,), jnp.float32)
        beta = jnp.zeros((OUT_F,), jnp.float32)
        return {'x': x, 'adj': adj, 'W': W, 'a': a, 'gamma': gamma, 'beta': beta}
    _L1_gnn_all = _L1_gnn_setup()
    _L1_gnn_in = {k: v for k, v in _L1_gnn_all.items() if k in ('W', 'a', 'gamma', 'beta')}
    del _L1_gnn_all

    def _L2_gnn_setup():
        import jax, jax.numpy as jnp
        import numpy as np
        N = 8192
        D = 128
        key = jax.random.key(seed)
        k1, k2, k3, k4 = jax.random.split(key, 4)
        x = jax.random.normal(k1, (N, D), dtype=jnp.float32)
        adj = jax.random.randint(k2, (N, N), 0, 2, dtype=jnp.int32)
        W = jax.random.normal(k3, (D, D), dtype=jnp.float32) * 0.05
        b = jax.random.normal(k4, (D,), dtype=jnp.float32) * 0.05
        return {'x': x, 'adj': adj, 'W': W, 'b': b}
    _L2_gnn_all = _L2_gnn_setup()
    _L2_gnn_in = {k: v for k, v in _L2_gnn_all.items() if k in ('W', 'b')}
    del _L2_gnn_all

    def _L3_gnn_setup():
        import jax, jax.numpy as jnp
        import numpy as np
        N, F_IN, F_OUT = (4096, 128, 128)
        ALPHA = 0.2
        NEG = -9000000000000000.0
        key = jax.random.key(seed)
        k1, k2, k3, k4, k5 = jax.random.split(key, 5)
        h = jax.random.normal(k1, (N, F_IN), dtype=jnp.float32)
        adj = jax.random.randint(k2, (N, N), 0, 2, dtype=jnp.int32)
        W_w = jax.random.normal(k3, (F_IN, F_OUT), dtype=jnp.float32) / np.sqrt(F_IN)
        W_b = jax.random.normal(k4, (F_OUT,), dtype=jnp.float32) * 0.01
        a = jax.random.normal(k5, (2 * F_OUT, 1), dtype=jnp.float32) / np.sqrt(2 * F_OUT)
        return {'h': h, 'adj': adj, 'W_w': W_w, 'W_b': W_b, 'a': a}
    _L3_gnn_all = _L3_gnn_setup()
    _L3_gnn_in = {k: v for k, v in _L3_gnn_all.items() if k in ('W_w', 'W_b', 'a')}
    del _L3_gnn_all
    return {'x': x, 'adj': adj, 'L0_gnn_W': _L0_gnn_in['W'], 'L0_gnn_a': _L0_gnn_in['a'], 'L1_gnn_W': _L1_gnn_in['W'], 'L1_gnn_a': _L1_gnn_in['a'], 'L1_gnn_gamma': _L1_gnn_in['gamma'], 'L1_gnn_beta': _L1_gnn_in['beta'], 'L2_gnn_W': _L2_gnn_in['W'], 'L2_gnn_b': _L2_gnn_in['b'], 'L3_gnn_W_w': _L3_gnn_in['W_w'], 'L3_gnn_W_b': _L3_gnn_in['W_b'], 'L3_gnn_a': _L3_gnn_in['a']}

def reference(x, adj, L0_gnn_W, L0_gnn_a, L1_gnn_W, L1_gnn_a, L1_gnn_gamma, L1_gnn_beta, L2_gnn_W, L2_gnn_b, L3_gnn_W_w, L3_gnn_W_b, L3_gnn_a):
    import jax
    import jax.numpy as jnp

    def _L0_gnn_ref(node, adj, W, a):
        import jax, jax.numpy as jnp
        import numpy as np
        NEG_INF = -9000000000000000.0
        h = node @ W
        Fdim = W.shape[0]
        s1 = h @ a[:Fdim, 0]
        s2 = h @ a[Fdim:, 0]
        e = jax.nn.leaky_relu(s1[:, None] + s2[None, :], negative_slope=0.01)
        e = jnp.where(adj > 0, e, jnp.float32(NEG_INF))
        att = jax.nn.softmax(e, axis=1)
        return h + att @ node

    def _L1_gnn_ref(x, adj, W, a, gamma, beta):
        import jax, jax.numpy as jnp
        import numpy as np
        N = 2048
        IN_F = 128
        OUT_F = 128
        HEADS = 4
        HEAD_DIM = OUT_F // HEADS
        ALPHA = 0.2
        NEG_INF = -9000000000000000.0
        LN_EPS = 1e-05
        n = x.shape[0]
        h = (x @ W).reshape(n, HEADS, HEAD_DIM)
        a1 = a[:HEAD_DIM, 0]
        a2 = a[HEAD_DIM:, 0]
        s = jnp.einsum('nhd,d->nh', h, a1) + jnp.einsum('nhd,d->nh', h, a2)
        s = jnp.where(s >= 0, s, ALPHA * s)
        e = jnp.broadcast_to(s[:, :, None], (n, HEADS, n))
        mask = adj[:, None, :] > 0
        e = jnp.where(mask, e, NEG_INF)
        attn = jax.nn.softmax(e, axis=-1)
        h_prime = jnp.einsum('ihj,jhd->ihd', attn, h).reshape(n, OUT_F)
        mu = jnp.mean(h_prime, axis=-1, keepdims=True)
        var = jnp.var(h_prime, axis=-1, keepdims=True)
        out = (h_prime - mu) * jax.lax.rsqrt(var + LN_EPS) * gamma + beta
        return out

    def _L2_gnn_ref(x, adj, W, b):
        import jax, jax.numpy as jnp
        import numpy as np
        N = 8192
        D = 128
        a = (adj == 1).astype(x.dtype)
        deg = jnp.sum(a, axis=1, keepdims=True)
        agg = jnp.einsum('ij,jf->if', a, x) / deg
        return agg @ W.T + b

    def _L3_gnn_ref(h, adj, W_w, W_b, a):
        import jax, jax.numpy as jnp
        import numpy as np
        N, F_IN, F_OUT = (4096, 128, 128)
        ALPHA = 0.2
        NEG = -9000000000000000.0
        Wh = h @ W_w + W_b
        a1 = a[:F_OUT, 0]
        a2 = a[F_OUT:, 0]
        e = jax.nn.leaky_relu((Wh @ a1)[:, None] + (Wh @ a2)[None, :], negative_slope=ALPHA)
        attention = jnp.where(adj > 0, e, NEG)
        attention = jax.nn.softmax(attention, axis=1)
        h_prime = attention @ Wh
        return h_prime
    x = _layernorm(x + _L0_gnn_ref(x, adj, L0_gnn_W, L0_gnn_a), axis=-1)
    x = _layernorm(x + _L1_gnn_ref(x, adj, L1_gnn_W, L1_gnn_a, L1_gnn_gamma, L1_gnn_beta), axis=-1)
    x = _layernorm(x + _L2_gnn_ref(x, adj, L2_gnn_W, L2_gnn_b), axis=-1)
    x = _layernorm(x + _L3_gnn_ref(x, adj, L3_gnn_W_w, L3_gnn_W_b, L3_gnn_a), axis=-1)
    return x

_drawn_inputs = setup_inputs


def setup_inputs(seed=0):
    import zlib

    import numpy as np

    out = dict(_drawn_inputs(seed))
    spreads = {'L1_gnn_gamma': (1.0, 0.2), 'L1_gnn_beta': (0.0, 0.1)}
    factors = {'L3_gnn_W_b': 8.0}
    for name, (base, spread) in spreads.items():
        noise = np.random.default_rng([zlib.crc32(name.encode()), seed]).standard_normal(out[name].shape)
        drawn = base * np.exp(spread * noise) if base else spread * noise
        out[name] = jnp.asarray(drawn.astype(out[name].dtype))
    for name, factor in factors.items():
        out[name] = (out[name] * factor).astype(out[name].dtype)
    return out
```

```python
import concourse.bass as bass
from concourse import mybir
from contextlib import ExitStack


F32 = mybir.dt.float32
F16 = mybir.dt.float16
F8 = mybir.dt.float8e5
I32 = mybir.dt.int32
U8 = mybir.dt.uint8
ALU = mybir.AluOpType
ACT = mybir.ActivationFunctionType
AX = mybir.AxisListType
RMAX = bass.bass_isa.ReduceOp.max

P = 128
BW = 2048
BANK = 512
SLOTS = 4
CAP = 80.0
EPS = 1e-5
CODE_OF_1 = 60.0
SPLIT = 4096.0


def graph_layers(nc, x, x_t, adj, w0, w0_t, a0, w1, gamma, beta, w2_t, b2, w3, w3_t, a3, b3, out):
    N, D = x.shape
    NT = N // P
    NB = N // BW
    BT = BW // P
    NQ = NT // SLOTS
    BK = BW // BANK

    with ExitStack() as ctx:
        def sb(name, shape, dt):
            return ctx.enter_context(nc.sbuf_tensor(name, shape, dt))

        def sem(name):
            return ctx.enter_context(nc.semaphore(name))

        code_dram = nc.dram_tensor("code_dram", [NB * NT, P, BW], U8, kind="Internal").ap()

        x_in = sb("x_in", [P, NT, D], F32)
        x_cur = sb("x_cur", [P, NT, D], F32)
        shared = sb("shared", [P, NT * D], F32)
        w_row = shared[:, :]
        parts = shared[:, :].bitcast(F16).rearrange("p (h t d) -> p h t d", h=2, t=NT)
        adj_sb = sb("adj_sb", [P, SLOTS, BW], I32)
        prob = sb("prob", [P, SLOTS, BW], F32)
        mask = prob[:, :, :].rearrange("p s w -> p (s w)").bitcast(F16)[:, 0:SLOTS * BW].rearrange(
            "p (s w) -> p s w", s=SLOTS)
        code = sb("code", [P, SLOTS, BW], U8)
        code_f8 = code[:, :, :].bitcast(F8)
        sums_t = sb("sums_t", [P, BW], F32)
        res = sb("res", [P, BT, D], F32)
        sq = sb("sq", [P, BW], F32)
        sq3 = sq[:, :].rearrange("p (t d) -> p t d", d=D)
        x_t_sb = [sums_t[:, :], sq[:, :]]
        xs = sb("xs", [P, SLOTS, D], F32)
        ident = sb("ident", [P, P], F32)
        ones = sb("ones", [P, P], F32)
        inv_n = sb("inv_n", [P, 1], F32)
        eps_c = sb("eps_c", [P, 1], F32)
        fold_t = sb("fold_t", [P, P], F32)
        proj = [sb(f"proj{n}", [P, D], F32) for n in range(4)]
        w_raw = sb("w_raw", [P, 4, D], F32)
        w_tr = [prob[:, n, 0:D] for n in range(2)]
        gamma_b = sb("gamma_b", [P, D], F32)
        beta_b = sb("beta_b", [P, D], F32)
        a_cols = sb("a_cols", [P, 4], F32)
        b3_col = sb("b3_col", [P, 1], F32)
        b_rows = sb("b_rows", [1, 2, D], F32)
        b3_wide = prob[:, 2, 0:D]
        sv0 = sb("sv0", [P, 3], F32)
        sv3 = sb("sv3", [P, 2], F32)
        c3 = sb("c3", [P, 2], F32)
        s_nat = sb("s_nat", [P, NT, 3], F32)
        x_part = sb("x_part", [P, NB, D], F32)
        mean_row = sb("mean_row", [1, D], F32)
        t_col = sb("t_col", [P, 1], F32)
        s_max = sb("s_max", [P, 2], F32)
        w_log = sb("w_log", [P, NT], F32)
        s2_rel = sb("s2_rel", [P, NT], F32)
        w_nat = sb("w_nat", [P, NT], F32)
        r_nat = sb("r_nat", [P, NT], F32)
        v_nat = sb("v_nat", [P, NT], F32)
        v_mean = sb("v_mean", [P, NT], F32)
        den = sb("den", [P, 3, BT], F32)
        stat = sb("stat", [P, 4, BT], F32)

        acc = ctx.enter_context(nc.psum_tensor("acc", [P, BK, BANK], F32))
        epi = [ctx.enter_context(nc.psum_tensor(f"epi{n}", [P, BANK], F32)) for n in range(2)]
        tr_ps = ctx.enter_context(nc.psum_tensor("tr_ps", [P, BANK], F32))
        small = ctx.enter_context(nc.psum_tensor("small", [P, BANK], F32))
        DEN = small[:, 0:BT]
        SNAT = small[:, 16:16 + 3 * BT].rearrange("p (t c) -> p t c", c=3)
        ROW = small[0:1, 128:256]
        COL = small[:, 256:257]

        weights_in = sem("weights_in")
        x_loaded = sem("x_loaded")
        x_t_in = [sem(f"x_t_in{n}") for n in range(2)]
        consts_ready = sem("consts_ready")
        fold_ready = sem("fold_ready")
        fold_products = sem("fold_products")
        weights_ready = sem("weights_ready")
        h_ready = sem("h_ready")
        h_used = sem("h_used")
        s0_ready = sem("s0_ready")
        s0_used = sem("s0_used")
        dve_chain = sem("dve_chain")
        adj_in = [sem(f"adj_in{k}") for k in range(SLOTS)]
        adj_coded = sem("adj_coded")
        code_stored = [sem(f"code_stored{k}") for k in range(SLOTS)]
        out_stored = sem("out_stored")

        named = {}

        def of(layer, name):
            key = f"l{layer}_{name}"
            if key not in named:
                named[key] = sem(key)
            return named[key]

        LAYERS = (0, 1, 2, 3)
        ATTENTION = {0: 0.01, 3: 0.2}
        MEAN_ROWS = (0, 1, 3)
        LAYER_NORMS = {0: 1, 1: 2, 2: 1, 3: 1}
        S_NEXT = {2: 2}

        block = ctx.enter_context(nc.Block())

        @block.sync
        def _(sp):
            for dst, src in ((w_raw[:, 0, :], w0), (w_tr[0], w0_t), (w_raw[:, 1, :], w1), (w_raw[:, 2, :], w2_t),
                             (w_raw[:, 3, :], w3), (w_tr[1], w3_t), (a_cols[:, 0:2], a0), (a_cols[:, 2:4], a3),
                             (b3_col[:, :], b3.rearrange("(d a) -> d a", a=1)),
                             (b_rows[0:1, 0, :], b2.rearrange("(a d) -> a d", a=1)),
                             (b_rows[0:1, 1, :], b3.rearrange("(a d) -> a d", a=1)),
                             (gamma_b[:, :], gamma.partition_broadcast(P)),
                             (beta_b[:, :], beta.partition_broadcast(P))):
                sp.dma_start(dst, src).then_inc(weights_in, 16)
            for n in range(2):
                sp.dma_start(x_t_sb[n], x_t[:, n * BW:(n + 1) * BW]).then_inc(x_t_in[n], 16)
            sp.dma_start(x_in[:, :, :], x.rearrange("(t p) d -> p t d", p=P)).then_inc(x_loaded, 16)
            for n in range(2):
                sp.wait_ge(s0_ready, n + 1)
                sp.dma_start(x_t_sb[n], x_t[:, (n + 2) * BW:(n + 3) * BW]).then_inc(x_t_in[n], 16)
            for k in range(SLOTS):
                sp.dma_start(adj_sb[:, k, :], adj[k]).then_inc(adj_in[k], 16)
            with sp.Fori(1, NB * NQ) as q:
                for k in range(SLOTS):
                    sp.wait_ge(of(0, "prob_ready"), (q - 1) * SLOTS + (k + 1))
                    sp.wait_ge(adj_coded, (q - 1) * SLOTS + (k + 1))
                    sp.dma_start(adj_sb[:, k, :], adj[q * SLOTS + k]).then_inc(adj_in[k], 16)
            for k in range(SLOTS):
                sp.wait_ge(code_stored[k], 16 * NB * NQ + 16)
            for layer in (1, 2, 3):
                for k in range(SLOTS):
                    if layer > 1:
                        sp.wait_ge(of(layer - 1, "prob_ready"), NB * NT)
                    sp.dma_start(code[:, k, :], code_dram[k]).then_inc(of(layer, f"code_in{k}"), 16)
                with sp.Fori(1, NB * NQ) as q:
                    for k in range(SLOTS):
                        sp.wait_ge(of(layer, "prob_ready"), (q - 1) * SLOTS + (k + 1))
                        sp.dma_start(code[:, k, :],
                                     code_dram[q * SLOTS + k]).then_inc(of(layer, f"code_in{k}"), 16)

        @block.gpsimd
        def _(pool):
            nc.gpsimd.memset(ones[:, :], 1.0).then_inc(consts_ready, 1)
            nc.gpsimd.memset(inv_n[:, :], 1.0 / N).then_inc(consts_ready, 1)
            nc.gpsimd.memset(eps_c[:, :], EPS).then_inc(consts_ready, 1)
            nc.gpsimd.memset(ident[:, :], 0.0).then_inc(consts_ready, 1)
            pool.wait_ge(consts_ready, 4)
            nc.gpsimd.affine_select(out=ident[:, :], in_=ident[:, :], compare_op=ALU.not_equal, fill=1.0, base=0,
                                    pattern=[[-1, P]], channel_multiplier=1).then_inc(consts_ready, 1)
            for layer in ATTENTION:
                pool.wait_ge(of(layer, "smax_ready"), 1)
                nc.gpsimd.partition_all_reduce(s_max[:, 1:2], s_max[:, 0:1], P, RMAX).then_inc(of(layer, "s_all"), 1)

        @block.scalar
        def _(act):
            def exps(layer):
                al = ATTENTION[layer]
                act.wait_ge(of(layer, "logs_ready"), 1)
                if layer:
                    act.wait_ge(of(layer - 1, "x_stored"), NB + 1)
                nc.scalar.activation(w_nat[:, :], w_log[:, :], ACT.Exp).then_inc(of(layer, "exps_ready"), 1)
                nc.scalar.activation(r_nat[:, :], s2_rel[:, :], ACT.Exp, scale=1.0 - al)\
                    .then_inc(of(layer, "exps_ready"), 1)
                nc.scalar.activation(v_nat[:, :], s2_rel[:, :], ACT.Exp, scale=al)\
                    .then_inc(of(layer, "exps_ready"), 1)

            def row_copies(layer):
                with act.Fori(0, NT // 8) as g:
                    for n in range(2):
                        act.wait_ge(of(layer, "row_ready"), g * 2 + (n + 1))
                        nc.scalar.copy(w_row[:, bass.ds((g * 2 + n) * BANK, BANK)], epi[n][:, :])\
                            .then_inc(of(layer, "row_copied"), 1)

            def stationary(layer, j, k, count):
                act.wait_ge(of(layer, "prob_used"), count)
                src = x_in if layer == 0 else x_cur
                nc.scalar.activation(xs[:, k, 1:D], src[:, j, 1:D], ACT.Identity, scale=v_nat[:, j],
                                     bias=v_mean[:, j]).then_inc(of(layer, "xs_ready"), 1)
                nc.scalar.copy(xs[:, k, 0:1], v_nat[:, j]).then_inc(of(layer, "xs_ready"), 1)

            def epilogue(layer, ib):
                act.wait_ge(of(layer, "prob_used"), ib * NT + (NT + SLOTS))
                for b in range(BK):
                    nc.scalar.copy(sums_t[:, b * BANK:(b + 1) * BANK], acc[:, b, :])\
                        .then_inc(of(layer, "sums_ready"), 1)
                for n in range(LAYER_NORMS[layer]):
                    c = ib * LAYER_NORMS[layer] + (n + 1)
                    act.wait_ge(of(layer, "centered"), c)
                    nc.scalar.activation(sq3, res[:, :, :], ACT.Square).then_inc(of(layer, "squared"), 1)
                    act.wait_ge(of(layer, "var_ready"), c)
                    nc.scalar.activation(stat[:, 2, :], stat[:, 1, :], ACT.Sqrt, scale=1.0 / D, bias=eps_c[:, 0:1])\
                        .then_inc(of(layer, "std_ready"), 1)
                act.wait_ge(of(layer, "res_ready"), ib + 1)
                if layer == 3:
                    act.dma_start(out.rearrange("(b t p) d -> b p t d", p=P, t=BT)[ib], res[:, :, :])\
                        .then_inc(out_stored, 16)
                else:
                    nc.scalar.copy(x_cur[:, bass.ds(ib * BT, BT), :], res[:, :, :]).then_inc(of(layer, "x_stored"), 1)
                if layer in S_NEXT:
                    for g in range(BK):
                        act.wait_ge(of(layer, "tr_ready"), ib * BK + (g + 1))
                        nc.scalar.copy(sq[:, g * BANK:(g + 1) * BANK], tr_ps[:, :])\
                            .then_inc(of(layer, "tr_copied"), 1)

            for k in range(SLOTS):
                act.sem_inc(code_stored[k], 16)
            for layer in LAYERS:
                if layer in ATTENTION:
                    exps(layer)
                    row_copies(layer)
                    act.wait_ge(of(layer, "bias_ready"), 1)
                    with act.Fori(0, NB) as ib:
                        with act.Fori(0, NQ) as q:
                            for k in range(SLOTS):
                                step = ib * NT + q * SLOTS + k
                                if layer == 0:
                                    act.wait_ge(adj_in[k], (ib * NQ + q) * 16 + 16)
                                    act.wait_ge(code_stored[k], (ib * NQ + q) * 16 + 16)
                                stationary(layer, bass.ds(q * SLOTS + k, 1), k, step + 1)
                                if layer == 0:
                                    nc.scalar.activation(code_f8[:, k, :], adj_sb[:, k, :], ACT.Relu, saturate=False)\
                                        .then_inc(adj_coded, 1)
                                if layer == 0:
                                    act.wait_ge(adj_coded, step + 1)
                                    act.dma_start(code_dram[step], code[:, k, :])\
                                        .then_inc(code_stored[k], 16)
                        epilogue(layer, ib)
                else:
                    act.wait_ge(of(layer - 1, "x_stored"), NB + 1)
                    with act.Fori(0, NB) as ib:
                        nc.scalar.activation(parts[:, 0, bass.ds(ib * BT, BT), 1:D], x_cur[:, bass.ds(ib * BT, BT), 1:D],
                                             ACT.Copy, scale=SPLIT).then_inc(of(layer, "hi_ready"), 1)
                    with act.Fori(0, NB) as ib:
                        epilogue(layer, ib)
            act.wait_ge(out_stored, 16 * NB + 16)

        @block.vector
        def _(dve):
            count = [0]

            def link(ins):
                count[0] += 1
                ins.then_inc(dve_chain, 1)
                dve.wait_ge(dve_chain, count[0])

            def prepare_weights():
                dve.wait_ge(consts_ready, 5)
                nc.vector.tensor_copy(fold_t[:, :], ident[:, :]).then_inc(fold_ready, 1)
                nc.vector.tensor_copy(proj[0][:, :], ident[:, :]).then_inc(fold_ready, 1)
                dve.wait_ge(fold_ready, 2)
                nc.vector.memset(fold_t[0:1, :], -1.0).then_inc(fold_ready, 1)
                nc.vector.memset(proj[0][:, 0:1], -1.0).then_inc(fold_ready, 1)
                dve.wait_ge(fold_ready, 4)
                nc.vector.memset(fold_t[0:1, 0:1], 0.0).then_inc(fold_ready, 1)
                nc.vector.memset(proj[0][0:1, 0:1], 0.0).then_inc(fold_ready, 1)
                dve.wait_ge(weights_in, 16 * 13)
                nc.vector.tensor_scalar(b3_wide, ones[:, :], b3_col[:, 0:1], None, ALU.mult).then_inc(fold_ready, 1)
                dve.wait_ge(fold_products, 1)
                link(nc.vector.tensor_scalar(proj[1][:, :], epi[0][:, 0:D], 1.0 / SPLIT, None, ALU.mult))
                link(nc.vector.tensor_scalar(proj[2][:, :], epi[0][:, D:2 * D], 1.0 / SPLIT, None, ALU.mult))
                link(nc.vector.tensor_copy(proj[3][:, :], epi[0][:, 2 * D:3 * D]))
                link(nc.vector.tensor_copy(proj[2][0:1, :], b_rows[0:1, 0, :]))
                link(nc.vector.tensor_copy(proj[3][0:1, :], b_rows[0:1, 1, :]))
                link(nc.vector.memset(sv0[:, 2:3], 1.0 / D))
                link(nc.vector.tensor_copy(sv0[:, 0:2], epi[1][:, 0:2]))
                link(nc.vector.tensor_copy(sv3[:, :], epi[1][:, 2:4]))
                nc.vector.tensor_copy(c3[:, :], epi[1][:, 4:6]).then_inc(weights_ready, 1)

            def first_products():
                dve.wait_ge(x_loaded, 16)
                for ib in range(NB):
                    for g in range(BK):
                        t = ib * BT + g * 4
                        dve.wait_ge(h_ready, ib * BK + g + 1)
                        nc.vector.tensor_tensor(x_cur[:, t:t + 4, :],
                                                epi[g % 2][:, :].rearrange("p (t d) -> p t d", d=D),
                                                x_in[:, t:t + 4, :], ALU.add).then_inc(h_used, 1)
                    dve.wait_ge(s0_ready, ib + 1)
                    nc.vector.tensor_copy(s_nat[:, ib * BT:(ib + 1) * BT, :], SNAT).then_inc(s0_used, 1)
                    nc.vector.tensor_reduce(x_part[:, ib, :], x_in[:, ib * BT:(ib + 1) * BT, :].rearrange("p t d -> p d t"),
                                            AX.X, ALU.add).then_inc(of(0, "sum_ready"), 1)

            def mean_row_copy(layer):
                if layer:
                    dve.wait_ge(of(layer, "col_ready"), 1)
                    nc.vector.tensor_copy(t_col[:, :], COL).then_inc(of(layer, "col_copied"), 1)
                dve.wait_ge(of(layer, "mean_product"), 1)
                if layer == 3:
                    nc.vector.tensor_tensor(mean_row[:, :], ROW, b_rows[0:1, 1, :], ALU.add)\
                        .then_inc(of(layer, "mean_ready"), 1)
                else:
                    nc.vector.tensor_copy(mean_row[:, :], ROW).then_inc(of(layer, "mean_ready"), 1)

            def attention_rows(layer):
                al = ATTENTION[layer]
                if layer == 0:
                    dve.wait_ge(s0_used, NB)
                else:
                    dve.wait_ge(of(2, "s_copied"), NB + 1)
                    for c in range(2):
                        link(nc.vector.tensor_scalar(s_nat[:, :, c], s_nat[:, :, c], c3[:, c:c + 1], None, ALU.add))
                nc.vector.tensor_reduce(s_max[:, 0:1], s_nat[:, :, 1], AX.X, ALU.max)\
                    .then_inc(of(layer, "smax_ready"), 1)
                dve.wait_ge(of(layer, "s_all"), 1)
                link(nc.vector.tensor_scalar(w_log[:, :], s_nat[:, :, 0], s_max[:, 1:2], 1.0 - al, ALU.add, ALU.mult))
                link(nc.vector.tensor_scalar(w_log[:, :], w_log[:, :], CAP, None, ALU.min))
                nc.vector.tensor_scalar(s2_rel[:, :], s_nat[:, :, 1], s_max[:, 1:2], None, ALU.subtract)\
                    .then_inc(of(layer, "logs_ready"), 1)
                dve.wait_ge(of(layer, "exps_ready"), 3)
                with dve.Fori(0, NT // 8) as g:
                    for n in range(2):
                        dve.wait_ge(of(layer, "row_copied"), g * 2 + (n + 1))
                        for k in range(4):
                            t = bass.ds(g * 8 + (n * 4 + k), 1)
                            nc.vector.tensor_scalar(prob[:, k, n * P:(n + 1) * P], ident[:, :], w_nat[:, t], None,
                                                    ALU.mult).then_inc(of(layer, "diag_ready"), 1)
                if layer == 0:
                    nc.vector.scalar_tensor_tensor(v_mean[:, :], v_nat[:, :], -1.0, s_nat[:, :, 2], ALU.mult,
                                                   ALU.mult).then_inc(of(layer, "bias_ready"), 1)
                else:
                    nc.vector.memset(v_mean[:, :], 0.0).then_inc(of(layer, "bias_ready"), 1)
                dve.wait_ge(of(layer, "row_copied"), NT // 4 + 2)
                dve.wait_ge(of(layer, "exps_ready"), 3)

            CHAIN = {0: 6, 1: 13, 2: 5, 3: 6}

            def epilogue(layer, ib):
                done = [0]

                def tie(ins):
                    done[0] += 1
                    ins.then_inc(of(layer, "chain"), 1)
                    dve.wait_ge(of(layer, "chain"), ib * CHAIN[layer] + done[0])

                mean_rows = layer in MEAN_ROWS
                dve.wait_ge(of(layer, "sums_ready"), ib * BK + 2 * BK)
                if mean_rows:
                    nc.vector.tensor_scalar(sq[0:1, :], sums_t[0:1, :], 0.0, None, ALU.is_equal)\
                        .then_inc(of(layer, "zrow_ready"), 1)
                dve.wait_ge(of(layer, "den_ready"), ib + 1)
                if mean_rows:
                    tie(nc.vector.tensor_scalar(den[:, 0, :], DEN, 0.0, None, ALU.is_equal))
                    tie(nc.vector.tensor_tensor(den[:, 1, :], den[:, 0, :], DEN, ALU.add))
                else:
                    tie(nc.vector.tensor_copy(den[:, 1, :], DEN))
                tie(nc.vector.reciprocal(den[:, 2, :], den[:, 1, :]))
                if layer == 3:
                    dve.wait_ge(out_stored, ib * 16 + 16)
                else:
                    dve.wait_ge(of(layer, "x_stored"), ib + 1)
                for g in range(BK):
                    dve.wait_ge(of(layer, "proj_ready"), ib * BK + (g + 1))
                    for k in range(4):
                        t = g * 4 + k
                        src = epi[g % 2][:, k * D:(k + 1) * D]
                        if layer == 1:
                            ins = nc.vector.tensor_scalar(res[:, t, :], src, den[:, 2, t:t + 1], None, ALU.mult)
                        else:
                            ins = nc.vector.scalar_tensor_tensor(
                                res[:, t, :], src, den[:, 2, t:t + 1],
                                x_cur[:, bass.ds(ib * BT + t, 1), :].rearrange("p a d -> p (a d)"), ALU.mult, ALU.add)
                    ins.then_inc(of(layer, "proj_read"), 1)
                dve.wait_ge(of(layer, "proj_read"), ib * BK + (BK + 2))
                norms = LAYER_NORMS[layer]
                for n in range(norms):
                    c = ib * norms + (n + 1)
                    tie(nc.vector.tensor_reduce(stat[:, 0, :], res[:, :, :], AX.X, ALU.add))
                    tie(nc.vector.tensor_scalar(stat[:, 0, :], stat[:, 0, :], -1.0 / D, None, ALU.mult))
                    nc.vector.tensor_tensor(res[:, :, :], res[:, :, :],
                                            stat[:, 0, :].unsqueeze(2).to_broadcast([P, BT, D]), ALU.add)\
                        .then_inc(of(layer, "centered"), 1)
                    dve.wait_ge(of(layer, "squared"), c)
                    nc.vector.tensor_reduce(stat[:, 1, :], sq3, AX.X, ALU.add).then_inc(of(layer, "var_ready"), 1)
                    dve.wait_ge(of(layer, "std_ready"), c)
                    tie(nc.vector.reciprocal(stat[:, 3, :], stat[:, 2, :]))
                    ins = nc.vector.tensor_tensor(res[:, :, :], res[:, :, :],
                                                  stat[:, 3, :].unsqueeze(2).to_broadcast([P, BT, D]), ALU.mult)
                    if n == norms - 1:
                        ins.then_inc(of(layer, "res_ready"), 1)
                    else:
                        tie(ins)
                        tie(nc.vector.tensor_tensor(res[:, :, :], res[:, :, :],
                                                    gamma_b[:, :].unsqueeze(1).to_broadcast([P, BT, D]), ALU.mult))
                        tie(nc.vector.tensor_tensor(res[:, :, :], res[:, :, :],
                                                    beta_b[:, :].unsqueeze(1).to_broadcast([P, BT, D]), ALU.add))
                        tie(nc.vector.tensor_tensor(res[:, :, :], res[:, :, :], x_cur[:, bass.ds(ib * BT, BT), :],
                                                    ALU.add))
                if layer + 1 in MEAN_ROWS:
                    dve.wait_ge(of(layer, "res_ready"), ib + 1)
                    nc.vector.tensor_reduce(x_part[:, bass.ds(ib, 1), :].rearrange("p a d -> p (a d)"),
                                            res[:, :, :].rearrange("p t d -> p d t"), AX.X, ALU.add)\
                        .then_inc(of(layer + 1, "sum_ready"), 1)
                if layer in S_NEXT:
                    dve.wait_ge(of(layer, "s_ready"), ib + 1)
                    nc.vector.tensor_copy(s_nat[:, bass.ds(ib * BT, BT), 0:2], SNAT[:, :, 0:2])\
                        .then_inc(of(layer, "s_copied"), 1)
                assert done[0] == CHAIN[layer], (layer, done[0])

            prepare_weights()
            first_products()
            for layer in LAYERS:
                if layer == 3:
                    dve.sem_inc(out_stored, 16)
                else:
                    dve.sem_inc(of(layer, "x_stored"), 1)
                if layer in ATTENTION:
                    mean_row_copy(layer)
                    attention_rows(layer)
                    raw = adj_sb if layer == 0 else code
                    raw_in = adj_in if layer == 0 else [of(3, f"code_in{k}") for k in range(SLOTS)]
                    with dve.Fori(0, NB) as ib:
                        with dve.Fori(0, NQ) as q:
                            for pair in range(0, SLOTS, 2):
                                step = ib * NT + q * SLOTS + pair
                                for k in range(pair, pair + 2):
                                    j = bass.ds(q * SLOTS + k, 1)
                                    dve.wait_ge(of(layer, "prob_used"), step + (k - pair + 1))
                                    nc.vector.tensor_scalar(prob[:, k, :], w_row[:, bass.ds(ib * BW, BW)], r_nat[:, j],
                                                            1.0, ALU.mult, ALU.max).then_inc(of(layer, "t_ready"), 1)
                                for k in range(pair, pair + 2):
                                    dve.wait_ge(of(layer, "t_ready"), step + (k - pair + 1))
                                    dve.wait_ge(raw_in[k], (ib * NQ + q) * 16 + 16)
                                    nc.vector.scalar_tensor_tensor(prob[:, k, :], raw[:, k, :], 0.0, prob[:, k, :],
                                                                   ALU.is_gt, ALU.mult)\
                                        .then_inc(of(layer, "prob_ready"), 1)
                        epilogue(layer, ib)
                else:
                    link(nc.vector.memset(parts[:, 0, :, 0:1], 1.0))
                    link(nc.vector.memset(parts[:, 1, :, 0:1], 0.0))
                    with dve.Fori(0, NB) as ib:
                        bt = bass.ds(ib * BT, BT)
                        dve.wait_ge(of(layer, "hi_ready"), ib + 1)
                        nc.vector.scalar_tensor_tensor(parts[:, 1, bt, 1:D], x_cur[:, bt, 1:D], SPLIT,
                                                       parts[:, 0, bt, 1:D], ALU.mult, ALU.subtract)\
                            .then_inc(of(layer, "lo_ready"), 1)
                    if layer == 1:
                        mean_row_copy(layer)
                    with dve.Fori(0, NB) as ib:
                        with dve.Fori(0, NQ) as q:
                            for k in range(SLOTS):
                                step = ib * NT + q * SLOTS + k
                                dve.wait_ge(of(layer, f"code_in{k}"), (ib * NQ + q) * 16 + 16)
                                dve.wait_ge(of(layer, "prob_used"), step + 1)
                                nc.vector.tensor_scalar(mask[:, k, :], code[:, k, :], 0.0 if layer == 1 else CODE_OF_1, None,
                                                        ALU.is_gt if layer == 1 else ALU.is_equal)\
                                    .then_inc(of(layer, "prob_ready"), 1)
                        epilogue(layer, ib)

        @block.tensor
        def _(pe):
            def prepare_weights():
                pe.wait_ge(weights_in, 16 * 13)
                pe.wait_ge(fold_ready, 7)
                for n in range(3):
                    nc.tensor.matmul(epi[0][:, n * D:(n + 1) * D], fold_t[:, :], w_raw[:, n + 1, :], start=True, stop=True)
                nc.tensor.matmul(epi[1][:, 0:2], w_tr[0], a_cols[:, 0:2], start=True, stop=True)
                nc.tensor.matmul(epi[1][:, 2:4], w_tr[1], a_cols[:, 2:4], start=True, stop=True)
                nc.tensor.matmul(epi[1][:, 4:6], b3_wide, a_cols[:, 2:4], start=True, stop=True)\
                    .then_inc(fold_products, 1)
                pe.wait_ge(weights_ready, 1)

            def first_products():
                for ib in range(NB):
                    n = ib % 2
                    pe.wait_ge(x_t_in[n], 16 * (ib // 2 + 1))
                    for g in range(BK):
                        if ib * BK + g >= 2:
                            pe.wait_ge(h_used, ib * BK + g - 1)
                        for k in range(4):
                            t = g * 4 + k
                            mm = nc.tensor.matmul(epi[g % 2][:, k * D:(k + 1) * D], x_t_sb[n][:, t * P:(t + 1) * P],
                                                  w_raw[:, 0, :], start=True, stop=True)
                        mm.then_inc(h_ready, 1)
                    if ib:
                        pe.wait_ge(s0_used, ib)
                    for t in range(BT):
                        mm = nc.tensor.matmul(SNAT[:, t, :], x_t_sb[n][:, t * P:(t + 1) * P], sv0[:, :],
                                              start=True, stop=True)
                    mm.then_inc(s0_ready, 1)

            def mean_products(layer):
                pe.wait_ge(of(layer, "sum_ready"), NB)
                if layer == 0:
                    pe.wait_ge(s0_used, NB)
                elif layer - 1 in S_NEXT:
                    pe.wait_ge(of(layer - 1, "s_copied"), NB + 1)
                if layer == 0:
                    for b in range(NB):
                        mm = nc.tensor.matmul(ROW, inv_n[:, :], x_part[:, b, :], start=(b == 0), stop=(b == NB - 1))
                    mm.then_inc(of(0, "mean_product"), 1)
                    return
                for b in range(NB):
                    mm = nc.tensor.matmul(COL, x_part[:, b, :], inv_n[:, :], start=(b == 0), stop=(b == NB - 1))
                mm.then_inc(of(layer, "col_ready"), 1)
                pe.wait_ge(of(layer, "col_copied"), 1)
                nc.tensor.matmul(ROW, t_col[:, :], w_raw[:, layer, :], start=True, stop=True)\
                    .then_inc(of(layer, "mean_product"), 1)

            def row_products(layer):
                pe.sem_inc(of(layer, "row_copied"), 2)
                with pe.Fori(0, NT // 8) as g:
                    for n in range(2):
                        pe.wait_ge(of(layer, "row_copied"), g * 2 + (n + 1))
                        for k in range(4):
                            pe.wait_ge(of(layer, "diag_ready"), g * 8 + (n * 4 + k + 1))
                            mm = nc.tensor.matmul(epi[n][:, k * P:(k + 1) * P], ones[:, :], prob[:, k, n * P:(n + 1) * P],
                                                  start=True, stop=True)
                        mm.then_inc(of(layer, "row_ready"), 1)

            def epilogue(layer, ib):
                mean_rows = layer in MEAN_ROWS
                pe.wait_ge(of(layer, "sums_ready"), ib * BK + 2 * BK)
                if layer in S_NEXT:
                    pe.wait_ge(of(layer, "s_copied"), ib + 1)
                for t in range(BT):
                    mm = nc.tensor.matmul(DEN[:, t:t + 1], sums_t[:, t * P:(t + 1) * P], ident[:, 0:1],
                                          start=True, stop=True)
                mm.then_inc(of(layer, "den_ready"), 1)
                if mean_rows:
                    pe.wait_ge(of(layer, "mean_ready"), 1)
                    pe.wait_ge(of(layer, "zrow_ready"), ib + 1)
                for g in range(BK):
                    pe.wait_ge(of(layer, "proj_read"), ib * BK + (g + 1))
                    for k in range(4):
                        t = g * 4 + k
                        o = epi[g % 2][:, k * D:(k + 1) * D]
                        mm = nc.tensor.matmul(o, sums_t[:, t * P:(t + 1) * P], proj[layer][:, :], start=True,
                                              stop=not mean_rows)
                        if mean_rows:
                            mm = nc.tensor.matmul(o, sq[0:1, t * P:(t + 1) * P], mean_row[:, :], start=False, stop=True)
                    mm.then_inc(of(layer, "proj_ready"), 1)
                if layer in S_NEXT:
                    pe.wait_ge(of(layer, "res_ready"), ib + 1)
                    for g in range(BK):
                        pe.wait_ge(of(layer, "tr_copied"), ib * BK + (g + 1))
                        for k in range(4):
                            mm = nc.tensor.transpose(tr_ps[:, k * P:(k + 1) * P], res[:, g * 4 + k, :], ident[:, :])
                        mm.then_inc(of(layer, "tr_ready"), 1)
                    pe.wait_ge(of(layer, "tr_copied"), ib * BK + (BK + 1))
                    for t in range(BT):
                        mm = nc.tensor.matmul(SNAT[:, t, 0:2], sq[:, t * P:(t + 1) * P], sv3[:, :], start=True, stop=True)
                    mm.then_inc(of(layer, "s_ready"), 1)

            def quad(layer, ib, q, first, last):
                for k in range(SLOTS):
                    step = ib * NT + q * SLOTS + k
                    pe.wait_ge(of(layer, "prob_ready"), step + 1)
                    start, stop = first and k == 0, last and k == SLOTS - 1
                    if layer in ATTENTION:
                        pe.wait_ge(of(layer, "xs_ready"), step * 2 + 2)
                        for b in range(BK):
                            mm = nc.tensor.matmul(acc[:, b, :], xs[:, k, :], prob[:, k, b * BANK:(b + 1) * BANK],
                                                  start=start, stop=stop)
                    else:
                        for h in range(2):
                            w = parts[:, h, bass.ds(q * SLOTS + k, 1), :].rearrange("p a d -> p (a d)")
                            for b in range(BK):
                                mm = nc.tensor.matmul(acc[:, b, :], w, mask[:, k, b * BANK:(b + 1) * BANK],
                                                      start=start and h == 0, stop=stop and h == 1)
                    mm.then_inc(of(layer, "prob_used"), 1)

            prepare_weights()
            first_products()
            for layer in LAYERS:
                if layer in MEAN_ROWS:
                    mean_products(layer)
                if layer in ATTENTION:
                    row_products(layer)
                else:
                    pe.wait_ge(of(layer, "lo_ready"), NB)
                pe.sem_inc(of(layer, "prob_used"), SLOTS)
                pe.sem_inc(of(layer, "proj_read"), 2)
                pe.sem_inc(of(layer, "sums_ready"), BK)
                if layer in S_NEXT:
                    pe.sem_inc(of(layer, "s_copied"), 1)
                    pe.sem_inc(of(layer, "tr_copied"), 1)
                with pe.Fori(0, NB) as ib:
                    pe.wait_ge(of(layer, "sums_ready"), ib * BK + BK)
                    quad(layer, ib, 0, True, False)
                    with pe.Fori(1, NQ - 1) as q:
                        quad(layer, ib, q, False, False)
                    quad(layer, ib, NQ - 1, False, True)
                    epilogue(layer, ib)


_LAYOUT = {
    "x": lambda i: i["x"],
    "x_t": lambda i: i["x"].T,
    "adj": lambda i: i["adj"].T.reshape(i["adj"].shape[1] // P, P, i["adj"].shape[0] // BW, BW)
    .transpose(2, 0, 1, 3).reshape(-1, P, BW),
    "w0": lambda i: i["L0_gnn_W"], "w0_t": lambda i: i["L0_gnn_W"].T,
    "a0": lambda i: i["L0_gnn_a"].reshape(2, -1).T,
    "w1": lambda i: i["L1_gnn_W"], "gamma": lambda i: i["L1_gnn_gamma"], "beta": lambda i: i["L1_gnn_beta"],
    "w2_t": lambda i: i["L2_gnn_W"].T, "b2": lambda i: i["L2_gnn_b"],
    "w3": lambda i: i["L3_gnn_W_w"], "w3_t": lambda i: i["L3_gnn_W_w"].T,
    "a3": lambda i: i["L3_gnn_a"].reshape(2, -1).T, "b3": lambda i: i["L3_gnn_W_b"],
}


def kernel(**inputs):
    import numpy as _np
    import concourse.bacc as _bacc
    from concourse import mybir as _mybir
    from concourse.bass_utils import run_bass_kernel_spmd as _run

    nc = _bacc.Bacc("TRN2", target_bir_lowering=False, num_devices=1)
    inputs = {name: _np.asarray(a) for name, a in inputs.items()}
    arrays, args = {}, []
    for name, lay in _LAYOUT.items():
        a = _np.ascontiguousarray(lay(inputs))
        arrays[f"in_{name}"] = a
        args.append(nc.dram_tensor(f"in_{name}", a.shape, _mybir.dt.from_np(a.dtype), kind="ExternalInput").ap())
    out = nc.dram_tensor("out_0", inputs["x"].shape, _mybir.dt.float32, kind="ExternalOutput").ap()
    graph_layers(nc, *args, out)
    r = _run(nc, [arrays], core_ids=[0])
    return r.results[0]["out_0"]
```

```python
import concourse.bass as bass
from concourse import mybir
from contextlib import ExitStack


F32 = mybir.dt.float32
F16 = mybir.dt.float16
F8 = mybir.dt.float8e5
I32 = mybir.dt.int32
U8 = mybir.dt.uint8
U16 = mybir.dt.uint16
ALU = mybir.AluOpType
ACT = mybir.ActivationFunctionType
AX = mybir.AxisListType
RMAX = bass.bass_isa.ReduceOp.max

P = 128
BW = 2048
BANK = 512
SLOTS = 4
QR = 4
CAP = 80.0
EPS = 1e-5
CODE_SCALE = 40.0
CODE_BIAS = 0.4054651 - CODE_SCALE
BIT_GT0 = 5
BIT_EQ1 = 1
BIT_2_M7 = 13
MR = 2
POS = 16
PLACES = {
    "attention": {"project_1": 0, "project_2": 3, "residual_1": 4, "residual_2": 7, "means_0": 8,
                  "deviations_0a": 9, "deviations_0b": 10, "scales_0": 12, "normalize_0a": 13, "normalize_0b": 14,
                  "put": 15, "next_s": 15, "finish": 15},
    "mask": {"project_1": 0, "project_2": 3, "residual_1": 4, "residual_2": 7, "means_0": 7,
             "deviations_0a": 8, "deviations_0b": 8, "scales_0": 10, "normalize_0a": 11, "normalize_0b": 11,
             "own_norm": 12, "means_1": 12, "deviations_1a": 13, "deviations_1b": 13, "scales_1": 15,
             "normalize_1a": 15, "normalize_1b": 15, "put": 12, "next_s": 12, "finish": 15},
}
GT = 3
EB = 3
SPLIT = 4096.0


def graph_layers(nc, x, x_t, adj, w0, w0_t, a0, w1, gamma, beta, w2_t, b2, w3, w3_t, a3, b3, out):
    N, D = x.shape
    NT = N // P
    NB = N // BW
    BT = BW // P
    NQ = NT // SLOTS
    TURNS = NQ // QR
    BK = BW // BANK
    NG = -(-BT // GT)

    with ExitStack() as ctx:
        def sb(name, shape, dt):
            return ctx.enter_context(nc.sbuf_tensor(name, shape, dt))

        def sem(name):
            return ctx.enter_context(nc.semaphore(name))

        code_dram = nc.dram_tensor("code_dram", [NB * NT, P, BW], U8, kind="Internal").ap()
        code_quads = code_dram.rearrange("(n s) p w -> n p s w", s=SLOTS)

        x_in = sb("x_in", [P, NT, D], F32)
        x_cur = sb("x_cur", [P, NT, D], F32)
        shared = sb("shared", [P, NT * D], F32)
        w_row = shared[:, :]
        parts = shared[:, :].bitcast(F16).rearrange("p (h t d) -> p h t d", h=2, t=NT)
        adj_sb = sb("adj_sb", [P, SLOTS, BW], I32)
        prob = sb("prob", [P, SLOTS, BW], F32)
        code = sb("code", [P, SLOTS, BW], U8)
        code_f8 = code[:, :, :].bitcast(F8)
        quads = adj_sb[:, :, :].rearrange("p s w -> p (s w)")
        quad_u8 = quads.bitcast(U8).rearrange("p (c s w) -> p c s w", c=QR, s=SLOTS)
        mask_u16 = prob[:, :, :].rearrange("p s w -> p (s w)").bitcast(U16).rearrange(
            "p (m s h w) -> p m s h w", m=MR, s=SLOTS, h=2)
        mask = prob[:, :, :].rearrange("p s w -> p (s w)").bitcast(F16).rearrange(
            "p (m s w) -> p m s w", m=MR, s=SLOTS)
        quad_u16 = quads.bitcast(U16).rearrange("p (c s w) -> p c s w", c=QR, s=SLOTS)
        sums_t = sb("sums_t", [P, BW], F32)
        res = sb("res", [P, BT, D], F32)
        sq = sb("sq", [P, BW], F32)
        sq3 = sq[:, :].rearrange("p (t d) -> p t d", d=D)
        x_t_sb = [prob[:, 3, :], res[:, :, :].rearrange("p t d -> p (t d)"), sq[:, :], sums_t[:, :]]
        diag = [prob[:, n, 0:BANK] for n in range(2)]
        xs = sb("xs", [P, SLOTS, D], F32)
        ident = sb("ident", [P, P], F32)
        ones = sb("ones", [P, P], F32)
        inv_n = sb("inv_n", [P, P], F32)
        eps_c = sb("eps_c", [P, 1], F32)
        minus_1 = sb("minus_1", [P, 1], F32)
        code_bias = sb("code_bias", [P, 1], F32)
        fold_t = sb("fold_t", [P, P], F32)
        proj = [sb(f"proj{n}", [P, D + 1], F32) for n in range(4)]
        w_raw = sb("w_raw", [P, 4, D], F32)
        w_tr = [prob[:, 2, n * D:(n + 1) * D] for n in range(2)]
        gamma_b = sb("gamma_b", [P, D], F32)
        beta_b = sb("beta_b", [P, D], F32)
        a_cols = sb("a_cols", [P, 4], F32)
        b3_col = sb("b3_col", [P, 1], F32)
        b2_row = sb("b2_row", [1, D], F32)
        b3_wide = prob[:, 2, 2 * D:3 * D]
        b3_b = sb("b3_b", [P, D], F32)
        sv0 = sb("sv0", [P, 3], F32)
        sv3 = sb("sv3", [P, 2], F32)
        c3 = sb("c3", [P, 2], F32)
        s_nat = sb("s_nat", [P, NT, 3], F32)
        x_part = sb("x_part", [P, NB, D], F32)
        mean_b = sb("mean_b", [P, D], F32)
        t_wide = fold_t[:, :]
        s_max = sb("s_max", [P, 2], F32)
        w_log = sb("w_log", [P, NT], F32)
        s2_rel = sb("s2_rel", [P, NT], F32)
        w_nat = sb("w_nat", [P, NT], F32)
        r_nat = sb("r_nat", [P, NT], F32)
        v_nat = sb("v_nat", [P, NT], F32)
        v_mean = sb("v_mean", [P, NT], F32)
        den = sb("den", [P, 4, BT], F32)
        stat = sb("stat", [P, 5, BT], F32)

        acc = ctx.enter_context(nc.psum_tensor("acc", [P, BK, BANK], F32))
        epi = [ctx.enter_context(nc.psum_tensor(f"epi{n}", [P, BANK], F32)) for n in range(EB)]
        small = ctx.enter_context(nc.psum_tensor("small", [P, BANK], F32))
        SNAT = small[:, 16:16 + 3 * BT].rearrange("p (t c) -> p t c", c=3)
        MEAN = small[:, 128:256]
        COL = small[:, 256:257]

        weights_in = sem("weights_in")
        x_loaded = sem("x_loaded")
        x_t_in = [sem(f"x_t_in{n}") for n in range(4)]
        consts_ready = sem("consts_ready")
        fold_ready = sem("fold_ready")
        fold_products = sem("fold_products")
        weights_ready = sem("weights_ready")
        h_ready = sem("h_ready")
        h_used = sem("h_used")
        s0_ready = sem("s0_ready")
        s0_used = sem("s0_used")
        dve_chain = sem("dve_chain")
        adj_in = [sem(f"adj_in{k}") for k in range(SLOTS)]
        adj_coded = sem("adj_coded")
        code_stored = [sem(f"code_stored{k}") for k in range(SLOTS)]
        out_stored = sem("out_stored")

        named = {}

        def of(layer, name):
            key = f"l{layer}_{name}"
            if key not in named:
                named[key] = sem(key)
            return named[key]

        LAYERS = (0, 1, 2, 3)
        ATTENTION = {0: 0.01, 3: 0.2}
        MEAN_ROWS = (0, 1, 3)
        LAYER_NORMS = {0: 1, 1: 2, 2: 1, 3: 1}
        S_NEXT = {2: 2}

        def is_at(index, n):
            return isinstance(index, int) and index == n

        def kind(layer):
            return "attention" if layer in ATTENTION else "mask"

        def blocks(eng, layer, quad, first_late, after_first, pieces, peel_last=False):
            straight = 1 if layer in ATTENTION else 2
            per_quad = POS // (straight * QR)

            def one(ib, late):
                for n in range(straight * QR):
                    quad(ib, n // QR, n % QR, late[n * per_quad:(n + 1) * per_quad])
                turn_ends = TURNS - 1 if peel_last else TURNS
                if turn_ends - straight > 1:
                    with eng.Fori(straight, turn_ends) as turn:
                        for c in range(QR):
                            quad(ib, turn, c, NOTHING)
                else:
                    for c in range(QR):
                        quad(ib, straight, c, NOTHING)
                if peel_last:
                    for c in range(QR):
                        quad(ib, TURNS - 1, c, NOTHING)

            one(0, first_late)
            after_first()
            with eng.Fori(1, NB) as ib:
                one(ib, placed(layer, pieces(ib - 1)))

        def nothing():
            pass

        NOTHING = [nothing] * POS

        def placed(layer, pieces):
            late = [[] for _ in range(POS)]
            for name, piece in pieces.items():
                late[PLACES[kind(layer)][name]].append(piece)
            return [lambda those=those: [piece() for piece in those] for those in late]

        block = ctx.enter_context(nc.Block())

        @block.sync
        def _(sp):
            for dst, src in ((w_raw[:, 0, :], w0), (w_tr[0], w0_t), (w_raw[:, 1, :], w1), (w_raw[:, 2, :], w2_t),
                             (w_raw[:, 3, :], w3), (w_tr[1], w3_t), (a_cols[:, 0:2], a0), (a_cols[:, 2:4], a3),
                             (b3_col[:, :], b3.rearrange("(d a) -> d a", a=1)),
                             (b2_row[:, :], b2.rearrange("(a d) -> a d", a=1)),
                             (b3_b[:, :], b3.partition_broadcast(P)),
                             (gamma_b[:, :], gamma.partition_broadcast(P)),
                             (beta_b[:, :], beta.partition_broadcast(P))):
                sp.dma_start(dst, src).then_inc(weights_in, 16)
            for n in range(NB):
                sp.dma_start(x_t_sb[n], x_t[:, n * BW:(n + 1) * BW]).then_inc(x_t_in[n], 16)
            sp.dma_start(x_in[:, :, :], x.rearrange("(t p) d -> p t d", p=P)).then_inc(x_loaded, 16)
            for k in range(SLOTS):
                sp.dma_start(adj_sb[:, k, :], adj[k]).then_inc(adj_in[k], 16)
            with sp.Fori(1, NB * NQ) as q:
                for k in range(SLOTS):
                    sp.wait_ge(of(0, "prob_ready"), (q - 1) * SLOTS + (k + 1))
                    sp.wait_ge(adj_coded, (q - 1) * SLOTS + (k + 1))
                    sp.dma_start(adj_sb[:, k, :], adj[q * SLOTS + k]).then_inc(adj_in[k], 16)
            for k in range(SLOTS):
                sp.wait_ge(code_stored[k], 16 * NB * NQ + 16)
            sp.wait_ge(of(0, "prob_ready"), NB * NT)
            for layer in (1, 2, 3):
                if layer > 1:
                    sp.wait_ge(of(layer - 1, "mask_ready"), NB * NQ)
                for c in range(QR):
                    sp.dma_start(quad_u8[:, c, :, :], code_quads[c]).then_inc(of(layer, f"code_in{c}"), 16)
                with sp.Fori(1, NB * TURNS) as turn:
                    for c in range(QR):
                        if layer in ATTENTION:
                            sp.wait_ge(of(layer, "prob_ready"), (turn - 1) * (QR * SLOTS) + (c + 1) * SLOTS)
                        else:
                            sp.wait_ge(of(layer, "mask_ready"), (turn - 1) * QR + (c + 1))
                        sp.dma_start(quad_u8[:, c, :, :], code_quads[turn * QR + c])\
                            .then_inc(of(layer, f"code_in{c}"), 16)

        @block.gpsimd
        def _(pool):
            nc.gpsimd.memset(ones[:, :], 1.0).then_inc(consts_ready, 1)
            nc.gpsimd.memset(inv_n[:, :], 1.0 / N).then_inc(consts_ready, 1)
            nc.gpsimd.memset(eps_c[:, :], EPS).then_inc(consts_ready, 1)
            nc.gpsimd.memset(minus_1[:, :], -1.0).then_inc(consts_ready, 1)
            nc.gpsimd.memset(code_bias[:, :], CODE_BIAS).then_inc(consts_ready, 1)
            nc.gpsimd.memset(ident[:, :], 0.0).then_inc(consts_ready, 1)
            pool.wait_ge(consts_ready, 6)
            nc.gpsimd.affine_select(out=ident[:, :], in_=ident[:, :], compare_op=ALU.not_equal, fill=1.0, base=0,
                                    pattern=[[-1, P]], channel_multiplier=1).then_inc(consts_ready, 1)
            for layer in ATTENTION:
                pool.wait_ge(of(layer, "smax_ready"), 1)
                nc.gpsimd.partition_all_reduce(s_max[:, 1:2], s_max[:, 0:1], P, RMAX).then_inc(of(layer, "s_all"), 1)

        @block.scalar
        def _(act):
            def exps(layer):
                al = ATTENTION[layer]
                act.wait_ge(of(layer, "logs_ready"), 1)
                if layer:
                    act.wait_ge(of(layer - 1, "x_stored"), NB + 1)
                nc.scalar.activation(w_nat[:, :], w_log[:, :], ACT.Exp).then_inc(of(layer, "exps_ready"), 1)
                nc.scalar.activation(r_nat[:, :], s2_rel[:, :], ACT.Exp, scale=1.0 - al)\
                    .then_inc(of(layer, "exps_ready"), 1)
                nc.scalar.activation(v_nat[:, :], s2_rel[:, :], ACT.Exp, scale=al)\
                    .then_inc(of(layer, "exps_ready"), 1)

            def row_copies(layer):
                with act.Fori(0, NT // 8) as g:
                    for n in range(2):
                        act.wait_ge(of(layer, "row_ready"), g * 2 + (n + 1))
                        nc.scalar.copy(w_row[:, bass.ds((g * 2 + n) * BANK, BANK)], epi[n][:, :])\
                            .then_inc(of(layer, "row_copied"), 1)

            def split_hi(layer, ib, stored):
                act.wait_ge(of(layer - 1, "x_stored"), stored)
                nc.scalar.activation(parts[:, 0, ib * BT:(ib + 1) * BT, 1:D], x_cur[:, ib * BT:(ib + 1) * BT, 1:D],
                                     ACT.Copy, scale=SPLIT).then_inc(of(layer, "hi_ready"), 1)

            def stationary(layer, j, k, count):
                act.wait_ge(of(layer, "prob_used"), count)
                src = x_in if layer == 0 else x_cur
                nc.scalar.activation(xs[:, k, 1:D], src[:, j, 1:D], ACT.Identity, scale=v_nat[:, j],
                                     bias=v_mean[:, j]).then_inc(of(layer, "xs_ready"), 1)
                nc.scalar.copy(xs[:, k, 0:1], v_nat[:, j]).then_inc(of(layer, "xs_ready"), 1)

            def take_sums(layer, ib):
                if layer in ATTENTION:
                    act.wait_ge(of(layer, "prob_used"), ib * NT + (NT + SLOTS))
                else:
                    act.wait_ge(of(layer, "quad_used"), ib * NQ + (NQ + MR))
                for b in range(BK):
                    nc.scalar.copy(sums_t[:, b * BANK:(b + 1) * BANK], acc[:, b, :])\
                        .then_inc(of(layer, "sums_ready"), 1)

            def pieces(layer, ib):
                norms = LAYER_NORMS[layer]

                def deviations(n, tiles):
                    act.wait_ge(of(layer, "means_ready"), ib * norms + (n + 1))
                    for t in tiles:
                        ins = nc.scalar.activation(sq3[:, t, :], res[:, t, :], ACT.Square, bias=stat[:, 0, t:t + 1],
                                                   accum_out=stat[:, 1, t:t + 1])
                    if tiles[-1] < BT - 1:
                        return
                    ins.then_inc(of(layer, "squared"), 1)
                    act.wait_ge(of(layer, "squared"), ib * norms + (n + 1))
                    nc.scalar.activation(stat[:, 2, :], stat[:, 1, :], ACT.Sqrt, scale=1.0 / D, bias=eps_c[:, 0:1])\
                        .then_inc(of(layer, "std_ready"), 1)

                def normalize(n, tiles):
                    act.wait_ge(of(layer, "scales_ready"), ib * norms + (n + 1))
                    to_x = layer == 0 or (layer == 1 and n == 1)
                    for t in tiles:
                        to = x_cur[:, bass.ds(ib * BT + t, 1), :].rearrange("p a d -> p (a d)") if to_x else res[:, t, :]
                        ins = nc.scalar.activation(to, res[:, t, :], ACT.Identity, scale=stat[:, 3, t:t + 1],
                                                   bias=stat[:, 4, t:t + 1])
                    if tiles[-1] == BT - 1:
                        ins.then_inc(of(layer, "x_stored" if to_x else "normed"), 1)

                def put_result():
                    act.wait_ge(of(layer, "normed"), ib + 1)
                    if layer == 3:
                        act.dma_start(out.rearrange("(b t p) d -> b p t d", p=P, t=BT)[ib], res[:, :, :])\
                            .then_inc(out_stored, 16)
                        return
                    nc.scalar.copy(x_cur[:, bass.ds(ib * BT, BT), :], res[:, :, :]).then_inc(of(layer, "x_stored"), 1)
                    for g in range(BK):
                        act.wait_ge(of(layer, "tr_ready"), ib * BK + (g + 1))
                        nc.scalar.copy(sq[:, g * BANK:(g + 1) * BANK], epi[g % EB][:, :])\
                            .then_inc(of(layer, "tr_copied"), 1)

                upper, lower = range(BT // 2), range(BT // 2, BT)
                late = {}
                for n in range(norms):
                    late[f"deviations_{n}a"] = lambda n=n: deviations(n, upper)
                    late[f"deviations_{n}b"] = lambda n=n: deviations(n, lower)
                    late[f"normalize_{n}a"] = lambda n=n: normalize(n, upper)
                    late[f"normalize_{n}b"] = lambda n=n: normalize(n, lower)
                if layer > 1:
                    late["put"] = put_result
                return late

            def attention_quad(layer, ib, turn, c, late):
                q = turn * QR + c
                for k in range(SLOTS):
                    step = ib * NT + q * SLOTS + k
                    j = bass.ds(q * SLOTS + k, 1)
                    if layer == 0:
                        act.wait_ge(adj_in[k], (ib * NQ + q) * 16 + 16)
                        act.wait_ge(code_stored[k], (ib * NQ + q) * 16 + 16)
                    stationary(layer, j, k, step + 1)
                    if layer == 0:
                        nc.scalar.activation(code_f8[:, k, :].rearrange("p (a h) -> p h a", h=2),
                                             adj_sb[:, k, :].rearrange("p (h a) -> p h a", h=2), ACT.Exp,
                                             scale=CODE_SCALE, bias=code_bias[:, 0:1], saturate=False)\
                            .then_inc(adj_coded, 1)
                        act.wait_ge(adj_coded, step + 1)
                        act.dma_start(code_dram[step], code[:, k, :]).then_inc(code_stored[k], 16)
                    else:
                        nc.scalar.activation(prob[:, k, :], w_row[:, bass.ds(ib * BW, BW)], ACT.Relu,
                                             scale=r_nat[:, j], bias=minus_1[:, 0:1]).then_inc(of(3, "t_ready"), 1)
                    if k == 1 and c == 0 and is_at(turn, 0) and not is_at(ib, 0):
                        take_sums(layer, ib - 1)
                    late[k]()

            def mask_quad(layer, ib, turn, c, late):
                if c == 0 and is_at(turn, 0) and not is_at(ib, 0):
                    take_sums(layer, ib - 1)
                if late is not NOTHING:
                    late[0]()
                    late[1]()

            act.wait_ge(consts_ready, 7)
            for k in range(SLOTS):
                act.sem_inc(code_stored[k], 16)
            for layer in LAYERS:
                if layer in ATTENTION:
                    exps(layer)
                    row_copies(layer)
                    act.wait_ge(of(layer, "bias_ready"), 1)
                    blocks(act, layer, lambda ib, turn, c, late: attention_quad(layer, ib, turn, c, late), NOTHING, nothing,
                           lambda ib: pieces(layer, ib))
                else:
                    take_sums(layer - 1, NB - 1)
                    for ib in range(NB - 1):
                        split_hi(layer, ib, NB)
                    late = placed(layer, pieces(layer - 1, NB - 1))
                    late[POS - 1] = lambda last=late[POS - 1]: (last(), split_hi(layer, NB - 1, NB + 1))
                    blocks(act, layer, lambda ib, turn, c, late: mask_quad(layer, ib, turn, c, late), late, nothing,
                           lambda ib: pieces(layer, ib))
                if layer >= 2:
                    take_sums(layer, NB - 1)
                    for piece in pieces(layer, NB - 1).values():
                        piece()
            act.wait_ge(out_stored, 16 * NB + 16)

        @block.vector
        def _(dve):
            count = [0]

            def link(ins):
                count[0] += 1
                ins.then_inc(dve_chain, 1)
                dve.wait_ge(dve_chain, count[0])

            def prepare_weights():
                dve.wait_ge(consts_ready, 7)
                nc.vector.tensor_copy(fold_t[:, :], ident[:, :]).then_inc(fold_ready, 1)
                nc.vector.tensor_copy(proj[0][:, 0:D], ident[:, :]).then_inc(fold_ready, 1)
                dve.wait_ge(fold_ready, 2)
                nc.vector.memset(fold_t[0:1, :], -1.0).then_inc(fold_ready, 1)
                nc.vector.memset(proj[0][:, 0:1], -1.0).then_inc(fold_ready, 1)
                dve.wait_ge(fold_ready, 4)
                nc.vector.memset(fold_t[0:1, 0:1], 0.0).then_inc(fold_ready, 1)
                nc.vector.memset(proj[0][0:1, 0:1], 0.0).then_inc(fold_ready, 1)
                for n in range(4):
                    link(nc.vector.tensor_copy(proj[n][:, D:D + 1], ident[:, 0:1]))
                dve.wait_ge(weights_in, 16 * 13)
                nc.vector.tensor_scalar(b3_wide, ones[:, :], b3_col[:, 0:1], None, ALU.mult).then_inc(fold_ready, 1)
                dve.wait_ge(fold_products, 1)
                link(nc.vector.tensor_scalar(proj[1][:, 0:D], epi[0][:, 0:D], 1.0 / SPLIT, None, ALU.mult))
                link(nc.vector.tensor_scalar(proj[2][:, 0:D], epi[0][:, D:2 * D], 1.0 / SPLIT, None, ALU.mult))
                link(nc.vector.tensor_copy(proj[3][:, 0:D], epi[0][:, 2 * D:3 * D]))
                link(nc.vector.tensor_copy(proj[2][0:1, 0:D], b2_row[:, :]))
                link(nc.vector.tensor_copy(proj[3][0:1, 0:D], b3_b[0:1, :]))
                link(nc.vector.memset(sv0[:, 2:3], 1.0 / D))
                link(nc.vector.tensor_copy(sv0[:, 0:2], epi[1][:, 0:2]))
                link(nc.vector.tensor_copy(sv3[:, :], epi[1][:, 2:4]))
                nc.vector.tensor_copy(c3[:, :], epi[1][:, 4:6]).then_inc(weights_ready, 1)

            def first_s():
                for ib in range(NB):
                    dve.wait_ge(s0_ready, ib + 1)
                    nc.vector.tensor_copy(s_nat[:, ib * BT:(ib + 1) * BT, :], SNAT).then_inc(s0_used, 1)

            def add_h(n):
                if n == 0:
                    dve.wait_ge(x_loaded, 16)
                dve.wait_ge(h_ready, n + 1)
                nc.vector.tensor_tensor(x_cur[:, 4 * n:4 * n + 4, :], epi[n % EB][:, :].rearrange("p (t d) -> p t d", d=D),
                                        x_in[:, 4 * n:4 * n + 4, :], ALU.add).then_inc(h_used, 1)

            def sum_x(ib):
                nc.vector.tensor_reduce(x_part[:, ib, :], x_in[:, ib * BT:(ib + 1) * BT, :].rearrange("p t d -> p d t"),
                                        AX.X, ALU.add).then_inc(of(0, "sum_ready"), 1)

            def mean_copy(layer):
                if layer:
                    dve.wait_ge(of(layer, "col_ready"), 1)
                    nc.vector.tensor_scalar(t_wide, ones[:, :], COL, None, ALU.mult)\
                        .then_inc(of(layer, "col_copied"), 1)
                dve.wait_ge(of(layer, "mean_product"), 1)
                if layer == 3:
                    ins = nc.vector.tensor_tensor(mean_b[:, :], MEAN, b3_b[:, :], ALU.add)
                else:
                    ins = nc.vector.tensor_copy(mean_b[:, :], MEAN)
                ins.then_inc(of(layer, "mean_ready"), 1)
                dve.wait_ge(of(layer, "mean_ready"), 1)

            def attention_rows(layer):
                al = ATTENTION[layer]
                if layer == 0:
                    dve.wait_ge(s0_used, NB)
                else:
                    dve.wait_ge(of(2, "s_copied"), NB + 1)
                    for c in range(2):
                        link(nc.vector.tensor_scalar(s_nat[:, :, c], s_nat[:, :, c], c3[:, c:c + 1], None, ALU.add))
                nc.vector.tensor_reduce(s_max[:, 0:1], s_nat[:, :, 1], AX.X, ALU.max)\
                    .then_inc(of(layer, "smax_ready"), 1)
                if layer == 0:
                    for n in range(BK):
                        add_h(n)
                dve.wait_ge(of(layer, "s_all"), 1)
                link(nc.vector.tensor_scalar(w_log[:, :], s_nat[:, :, 0], s_max[:, 1:2], 1.0 - al, ALU.add, ALU.mult))
                link(nc.vector.tensor_scalar(w_log[:, :], w_log[:, :], CAP, None, ALU.min))
                nc.vector.tensor_scalar(s2_rel[:, :], s_nat[:, :, 1], s_max[:, 1:2], None, ALU.subtract)\
                    .then_inc(of(layer, "logs_ready"), 1)
                dve.wait_ge(of(layer, "exps_ready"), 3)
                with dve.Fori(0, NT // 8) as g:
                    for n in range(2):
                        dve.wait_ge(of(layer, "row_copied"), g * 2 + (n + 1))
                        for k in range(4):
                            t = bass.ds(g * 8 + (n * 4 + k), 1)
                            nc.vector.tensor_scalar(diag[n][:, k * P:(k + 1) * P], ident[:, :], w_nat[:, t], None,
                                                    ALU.mult).then_inc(of(layer, "diag_ready"), 1)
                if layer == 0:
                    nc.vector.scalar_tensor_tensor(v_mean[:, :], v_nat[:, :], -1.0, s_nat[:, :, 2], ALU.mult,
                                                   ALU.mult).then_inc(of(layer, "bias_ready"), 1)
                else:
                    nc.vector.memset(v_mean[:, :], 0.0).then_inc(of(layer, "bias_ready"), 1)
                dve.wait_ge(of(layer, "row_copied"), NT // 4 + 2)
                dve.wait_ge(of(layer, "exps_ready"), 3)

            CHAIN = {0: 16, 1: 21, 2: 10, 3: 16}

            def pieces(layer, ib):
                done = [0]
                mean_rows = layer in MEAN_ROWS
                norms = LAYER_NORMS[layer]

                def mark(ins):
                    done[0] += 1
                    ins.then_inc(of(layer, "chain"), 1)

                def tie(ins):
                    mark(ins)
                    dve.wait_ge(of(layer, "chain"), ib * CHAIN[layer] + done[0])

                def residual(groups):
                    t0, t1 = groups[0] * GT, min(groups[-1] * GT + GT, BT)
                    for g in groups:
                        dve.wait_ge(of(layer, "proj_ready"), ib * NG + (g + 1))
                        n = min(GT, BT - g * GT)
                        mark(nc.vector.tensor_copy(
                            den[:, 0, g * GT:g * GT + n],
                            epi[g % EB][:, 0:n * (D + 1)].rearrange("p (k c) -> p k c", c=D + 1)[:, :, D]))
                    dve.wait_ge(of(layer, "chain"), ib * CHAIN[layer] + done[0])
                    full = 0
                    if mean_rows:
                        tie(nc.vector.tensor_scalar(den[:, 1, t0:t1], den[:, 0, t0:t1], 0.0, None, ALU.is_equal))
                        tie(nc.vector.tensor_tensor(den[:, 2, t0:t1], den[:, 0, t0:t1], den[:, 1, t0:t1], ALU.add))
                        full = 2
                    tie(nc.vector.reciprocal(den[:, 3, t0:t1], den[:, full, t0:t1]))
                    if groups[0] == 0:
                        if layer == 3:
                            dve.wait_ge(out_stored, ib * 16 + 16)
                        else:
                            dve.wait_ge(of(layer, "x_stored"), ib + 1)
                    for g in groups:
                        for t in range(g * GT, min(g * GT + GT, BT)):
                            k = t - g * GT
                            src = epi[g % EB][:, k * (D + 1):k * (D + 1) + D]
                            if layer == 1:
                                ins = nc.vector.tensor_scalar(res[:, t, :], src, den[:, 3, t:t + 1], None, ALU.mult)
                            else:
                                ins = nc.vector.scalar_tensor_tensor(
                                    res[:, t, :], src, den[:, 3, t:t + 1],
                                    x_cur[:, bass.ds(ib * BT + t, 1), :].rearrange("p a d -> p (a d)"), ALU.mult, ALU.add)
                        ins.then_inc(of(layer, "proj_read"), 1)

                def finish_residual():
                    dve.wait_ge(of(layer, "proj_read"), ib * NG + (NG + EB))
                    if mean_rows:
                        tie(nc.vector.tensor_tensor(sq3, den[:, 1, :].unsqueeze(2).to_broadcast([P, BT, D]),
                                                    mean_b[:, :].unsqueeze(1).to_broadcast([P, BT, D]), ALU.mult))
                        tie(nc.vector.tensor_tensor(res[:, :, :], res[:, :, :], sq3, ALU.add))

                def means():
                    tie(nc.vector.tensor_reduce(stat[:, 4, :], res[:, :, :], AX.X, ALU.add))
                    nc.vector.tensor_scalar(stat[:, 0, :], stat[:, 4, :], -1.0 / D, None, ALU.mult)\
                        .then_inc(of(layer, "means_ready"), 1)

                def scales(n):
                    dve.wait_ge(of(layer, "std_ready"), ib * norms + (n + 1))
                    tie(nc.vector.reciprocal(stat[:, 3, :], stat[:, 2, :]))
                    nc.vector.tensor_tensor(stat[:, 4, :], stat[:, 3, :], stat[:, 0, :], ALU.mult)\
                        .then_inc(of(layer, "scales_ready"), 1)

                def own_norm():
                    dve.wait_ge(of(layer, "normed"), ib + 1)
                    tie(nc.vector.tensor_tensor(res[:, :, :], res[:, :, :],
                                                gamma_b[:, :].unsqueeze(1).to_broadcast([P, BT, D]), ALU.mult))
                    tie(nc.vector.tensor_tensor(res[:, :, :], res[:, :, :],
                                                beta_b[:, :].unsqueeze(1).to_broadcast([P, BT, D]), ALU.add))
                    tie(nc.vector.tensor_tensor(res[:, :, :], res[:, :, :], x_cur[:, bass.ds(ib * BT, BT), :], ALU.add))

                def finish():
                    if layer + 1 in MEAN_ROWS:
                        dve.wait_ge(of(layer, "x_stored"), ib + 2)
                        nc.vector.tensor_reduce(x_part[:, bass.ds(ib, 1), :].rearrange("p a d -> p (a d)"),
                                                x_cur[:, bass.ds(ib * BT, BT), :].rearrange("p t d -> p d t"),
                                                AX.X, ALU.add).then_inc(of(layer + 1, "sum_ready"), 1)
                    if layer in S_NEXT:
                        dve.wait_ge(of(layer, "s_ready"), ib + 1)
                        nc.vector.tensor_copy(s_nat[:, bass.ds(ib * BT, BT), 0:2], SNAT[:, :, 0:2])\
                            .then_inc(of(layer, "s_copied"), 1)
                    assert done[0] == CHAIN[layer], (layer, done[0])

                def second_residual():
                    residual(range(EB, NG))
                    finish_residual()

                late = {"residual_1": lambda: residual(range(EB)), "residual_2": second_residual, "means_0": means,
                        "scales_0": lambda: scales(0)}
                if norms == 2:
                    late.update(own_norm=own_norm, means_1=means, scales_1=lambda: scales(1))
                late["finish"] = finish
                return late

            def adjacency_quad(ib, turn, c, late):
                q = turn * QR + c
                for pair in range(0, SLOTS, 2):
                    step = ib * NT + q * SLOTS + pair
                    for k in range(pair, pair + 2):
                        j = bass.ds(q * SLOTS + k, 1)
                        dve.wait_ge(of(0, "prob_used"), step + (k - pair + 1))
                        nc.vector.tensor_scalar(prob[:, k, :], w_row[:, bass.ds(ib * BW, BW)], r_nat[:, j],
                                                1.0, ALU.mult, ALU.max).then_inc(of(0, "t_ready"), 1)
                    for k in range(pair, pair + 2):
                        dve.wait_ge(of(0, "t_ready"), step + (k - pair + 1))
                        dve.wait_ge(adj_in[k], (ib * NQ + q) * 16 + 16)
                        nc.vector.scalar_tensor_tensor(prob[:, k, :], adj_sb[:, k, :], 0.0, prob[:, k, :],
                                                       ALU.is_gt, ALU.mult).then_inc(of(0, "prob_ready"), 1)
                    late[pair]()
                    late[pair + 1]()

            def codes_in(layer, ib, turn, c):
                dve.wait_ge(of(layer, f"code_in{c}"), (ib * TURNS + turn) * 16 + 16)

            def mask_quad(layer, ib, turn, c, late):
                bit = BIT_EQ1 if layer == 2 else BIT_GT0
                codes_in(layer, ib, turn, c)
                dve.wait_ge(of(layer, "quad_used"), ib * NQ + turn * QR + (c + 1))
                nc.vector.tensor_scalar(mask_u16[:, c % MR, :, 0, :], quad_u16[:, c, :, :], 1 << bit, BIT_2_M7 - bit,
                                        ALU.bitwise_and, ALU.logical_shift_left)
                nc.vector.tensor_scalar(mask_u16[:, c % MR, :, 1, :], quad_u16[:, c, :, :], 1 << (bit + 8),
                                        BIT_2_M7 - bit - 8, ALU.bitwise_and, ALU.logical_shift_left)\
                    .then_inc(of(layer, "mask_ready"), 1)
                if late is not NOTHING:
                    late[0]()
                    late[1]()

            def attention_quad(ib, turn, c, late):
                q = turn * QR + c
                codes_in(3, ib, turn, c)
                nc.vector.tensor_scalar(quad_u16[:, c, :, :], quad_u16[:, c, :, :], 0x101 << BIT_GT0, None,
                                        ALU.bitwise_and).then_inc(of(3, "mask_ready"), 1)
                dve.wait_ge(of(3, "mask_ready"), ib * NQ + q + 1)
                for k in range(SLOTS):
                    dve.wait_ge(of(3, "t_ready"), ib * NT + q * SLOTS + (k + 1))
                    halves = prob[:, k, :].rearrange("p (h a) -> p h a", h=2)
                    nc.vector.scalar_tensor_tensor(halves, halves, 1.0,
                                                   quad_u8[:, c, k, :].rearrange("p (a h) -> p h a", h=2),
                                                   ALU.add, ALU.mult).then_inc(of(3, "prob_ready"), 1)
                    late[k]()

            def split_lo(layer, ib):
                bt = slice(ib * BT, (ib + 1) * BT)
                dve.wait_ge(of(layer, "hi_ready"), ib + 1)
                nc.vector.scalar_tensor_tensor(parts[:, 1, bt, 1:D], x_cur[:, bt, 1:D], SPLIT, parts[:, 0, bt, 1:D],
                                               ALU.mult, ALU.subtract).then_inc(of(layer, "lo_ready"), 1)

            prepare_weights()
            first_s()
            for layer in LAYERS:
                if layer == 3:
                    dve.sem_inc(out_stored, 16)
                else:
                    dve.sem_inc(of(layer, "x_stored"), 1)
                after_first = (lambda: mean_copy(layer)) if layer in MEAN_ROWS else nothing
                if layer in ATTENTION:
                    attention_rows(layer)
                    late = NOTHING
                    if layer == 0:
                        late = [lambda n=n: sum_x(n) if n < NB else add_h(n) for n in range(POS)]
                    blocks(dve, layer, adjacency_quad if layer == 0 else attention_quad, late, after_first,
                           lambda ib: pieces(layer, ib))
                else:
                    dve.wait_ge(of(layer, "hi_ready"), 1)
                    link(nc.vector.memset(parts[:, 0, :, 0:1], 1.0))
                    link(nc.vector.memset(parts[:, 1, :, 0:1], 0.0))
                    for ib in range(NB - 1):
                        split_lo(layer, ib)
                    late = placed(layer, pieces(layer - 1, NB - 1))
                    late[POS - 1] = lambda last=late[POS - 1]: (last(), split_lo(layer, NB - 1))
                    blocks(dve, layer, lambda ib, turn, c, late: mask_quad(layer, ib, turn, c, late), late, after_first,
                           lambda ib: pieces(layer, ib))
                if layer >= 2:
                    for piece in pieces(layer, NB - 1).values():
                        piece()

        @block.tensor
        def _(pe):
            def prepare_weights():
                pe.wait_ge(weights_in, 16 * 13)
                pe.wait_ge(fold_ready, 7)
                for n in range(3):
                    nc.tensor.matmul(epi[0][:, n * D:(n + 1) * D], fold_t[:, :], w_raw[:, n + 1, :], start=True, stop=True)
                nc.tensor.matmul(epi[1][:, 0:2], w_tr[0], a_cols[:, 0:2], start=True, stop=True)
                nc.tensor.matmul(epi[1][:, 2:4], w_tr[1], a_cols[:, 2:4], start=True, stop=True)
                nc.tensor.matmul(epi[1][:, 4:6], b3_wide, a_cols[:, 2:4], start=True, stop=True)\
                    .then_inc(fold_products, 1)
                pe.wait_ge(weights_ready, 1)

            def first_s():
                for ib in range(NB):
                    pe.wait_ge(x_t_in[ib], 16)
                    if ib:
                        pe.wait_ge(s0_used, ib)
                    for t in range(BT):
                        mm = nc.tensor.matmul(SNAT[:, t, :], x_t_sb[ib][:, t * P:(t + 1) * P], sv0[:, :],
                                              start=True, stop=True)
                    mm.then_inc(s0_ready, 1)

            def h_products(n):
                if n >= EB:
                    pe.wait_ge(h_used, n - EB + 1)
                if n == BK:
                    pe.wait_ge(of(0, "row_copied"), NT // 4 + 2)
                for k in range(4):
                    t = n % BK * 4 + k
                    mm = nc.tensor.matmul(epi[n % EB][:, k * D:(k + 1) * D], x_t_sb[n // BK][:, t * P:(t + 1) * P],
                                          w_raw[:, 0, :], start=True, stop=True)
                mm.then_inc(h_ready, 1)

            def mean_products(layer):
                pe.wait_ge(of(layer, "sum_ready"), NB)
                if layer == 0:
                    pe.wait_ge(s0_used, NB)
                    for b in range(NB):
                        mm = nc.tensor.matmul(MEAN, inv_n[:, :], x_part[:, b, :], start=(b == 0), stop=(b == NB - 1))
                    mm.then_inc(of(0, "mean_product"), 1)
                    return
                if layer - 1 in S_NEXT:
                    pe.wait_ge(of(layer - 1, "s_copied"), NB + 1)
                for b in range(NB):
                    mm = nc.tensor.matmul(COL, x_part[:, b, :], inv_n[:, 0:1], start=(b == 0), stop=(b == NB - 1))
                mm.then_inc(of(layer, "col_ready"), 1)
                pe.wait_ge(of(layer, "col_copied"), 1)
                nc.tensor.matmul(MEAN, t_wide, w_raw[:, layer, :], start=True, stop=True)\
                    .then_inc(of(layer, "mean_product"), 1)

            def row_products(layer):
                if layer == 0:
                    pe.wait_ge(h_used, BK)
                else:
                    pe.wait_ge(of(2, "s_copied"), NB + 1)
                pe.sem_inc(of(layer, "row_copied"), 2)
                with pe.Fori(0, NT // 8) as g:
                    for n in range(2):
                        pe.wait_ge(of(layer, "row_copied"), g * 2 + (n + 1))
                        pe.wait_ge(of(layer, "diag_ready"), g * 8 + (n * 4 + 4))
                        nc.tensor.matmul(epi[n][:, :], ones[:, :], diag[n], start=True, stop=True)\
                            .then_inc(of(layer, "row_ready"), 1)

            def pieces(layer, ib):
                def project(groups):
                    if groups[0] == 0:
                        pe.wait_ge(of(layer, "sums_ready"), ib * BK + 2 * BK)
                        if layer in S_NEXT:
                            pe.wait_ge(of(layer, "s_copied"), ib + 1)
                    for g in groups:
                        pe.wait_ge(of(layer, "proj_read"), ib * NG + (g + 1))
                        for t in range(g * GT, min(g * GT + GT, BT)):
                            k = t - g * GT
                            mm = nc.tensor.matmul(epi[g % EB][:, k * (D + 1):(k + 1) * (D + 1)],
                                                  sums_t[:, t * P:(t + 1) * P], proj[layer][:, :], start=True, stop=True)
                        mm.then_inc(of(layer, "proj_ready"), 1)

                def next_s():
                    pe.wait_ge(of(layer, "normed"), ib + 1)
                    for g in range(BK):
                        if g >= EB:
                            pe.wait_ge(of(layer, "tr_copied"), ib * BK + (g - EB + 1))
                        for k in range(4):
                            mm = nc.tensor.transpose(epi[g % EB][:, k * P:(k + 1) * P], res[:, g * 4 + k, :], ident[:, :])
                        mm.then_inc(of(layer, "tr_ready"), 1)
                    pe.wait_ge(of(layer, "tr_copied"), ib * BK + BK)
                    for t in range(BT):
                        mm = nc.tensor.matmul(SNAT[:, t, 0:2], sq[:, t * P:(t + 1) * P], sv3[:, :], start=True, stop=True)
                    mm.then_inc(of(layer, "s_ready"), 1)

                late = {"project_1": lambda: project(range(EB)), "project_2": lambda: project(range(EB, NG))}
                if layer in S_NEXT:
                    late["next_s"] = next_s
                return late

            def quad(layer, ib, turn, c, late):
                q = turn * QR + c
                first, last = is_at(turn, 0) and c == 0, is_at(turn, TURNS - 1) and c == QR - 1
                if layer not in ATTENTION:
                    pe.wait_ge(of(layer, "mask_ready"), ib * NQ + q + 1)
                    if is_at(ib, 0) and c == 0:
                        pe.wait_ge(of(layer, "lo_ready"), turn + 1)
                for k in range(SLOTS):
                    step = ib * NT + q * SLOTS + k
                    start, stop = first and k == 0, last and k == SLOTS - 1
                    if layer in ATTENTION:
                        pe.wait_ge(of(layer, "prob_ready"), step + 1)
                        pe.wait_ge(of(layer, "xs_ready"), step * 2 + 2)
                    for h in range(1 if layer in ATTENTION else 2):
                        for b in range(BK):
                            if start and h == 0:
                                pe.wait_ge(of(layer, "sums_ready"), ib * BK + (b + 1))
                            if layer in ATTENTION:
                                mm = nc.tensor.matmul(acc[:, b, :], xs[:, k, :], prob[:, k, b * BANK:(b + 1) * BANK],
                                                      start=start, stop=stop)
                            else:
                                w = parts[:, h, bass.ds(q * SLOTS + k, 1), :].rearrange("p a d -> p (a d)")
                                mm = nc.tensor.matmul(acc[:, b, :], w, mask[:, c % MR, k, b * BANK:(b + 1) * BANK],
                                                      start=start and h == 0, stop=stop and h == 1)
                    if layer in ATTENTION:
                        mm.then_inc(of(layer, "prob_used"), 1)
                    elif k == SLOTS - 1:
                        mm.then_inc(of(layer, "quad_used"), 1)
                    if layer in ATTENTION:
                        late[k]()
                    elif k % 2 and late is not NOTHING:
                        late[k // 2]()

            prepare_weights()
            first_s()
            for n in range(BK):
                h_products(n)
            for layer in LAYERS:
                if layer in ATTENTION:
                    row_products(layer)
                    pe.sem_inc(of(layer, "prob_used"), SLOTS)
                else:
                    pe.sem_inc(of(layer, "quad_used"), MR)
                if layer:
                    pe.wait_ge(of(layer - 1, "sums_ready"), NB * BK + BK)
                pe.sem_inc(of(layer, "proj_read"), EB)
                pe.sem_inc(of(layer, "sums_ready"), BK)
                if layer in S_NEXT:
                    pe.sem_inc(of(layer, "s_copied"), 1)
                late = NOTHING
                if layer == 0:
                    late = [lambda n=n: h_products(n + BK - 1) if 1 <= n <= NT // 4 - BK else None for n in range(POS)]
                elif layer < 3:
                    late = placed(layer, pieces(layer - 1, NB - 1))
                blocks(pe, layer, lambda ib, turn, c, late: quad(layer, ib, turn, c, late), late,
                       (lambda: mean_products(layer)) if layer in MEAN_ROWS else nothing,
                       lambda ib: pieces(layer, ib), peel_last=True)
                if layer >= 2:
                    for piece in pieces(layer, NB - 1).values():
                        piece()


_LAYOUT = {
    "x": lambda i: i["x"],
    "x_t": lambda i: i["x"].T,
    "adj": lambda i: i["adj"].T.reshape(i["adj"].shape[1] // P, P, i["adj"].shape[0] // BW, BW)
    .transpose(2, 0, 1, 3).reshape(-1, P, BW),
    "w0": lambda i: i["L0_gnn_W"], "w0_t": lambda i: i["L0_gnn_W"].T,
    "a0": lambda i: i["L0_gnn_a"].reshape(2, -1).T,
    "w1": lambda i: i["L1_gnn_W"], "gamma": lambda i: i["L1_gnn_gamma"], "beta": lambda i: i["L1_gnn_beta"],
    "w2_t": lambda i: i["L2_gnn_W"].T, "b2": lambda i: i["L2_gnn_b"],
    "w3": lambda i: i["L3_gnn_W_w"], "w3_t": lambda i: i["L3_gnn_W_w"].T,
    "a3": lambda i: i["L3_gnn_a"].reshape(2, -1).T, "b3": lambda i: i["L3_gnn_W_b"],
}


def kernel(**inputs):
    import numpy as _np
    import concourse.bacc as _bacc
    from concourse import mybir as _mybir
    from concourse.bass_utils import run_bass_kernel_spmd as _run

    nc = _bacc.Bacc("TRN2", target_bir_lowering=False, num_devices=1)
    inputs = {name: _np.asarray(a) for name, a in inputs.items()}
    arrays, args = {}, []
    for name, lay in _LAYOUT.items():
        a = _np.ascontiguousarray(lay(inputs))
        arrays[f"in_{name}"] = a
        args.append(nc.dram_tensor(f"in_{name}", a.shape, _mybir.dt.from_np(a.dtype), kind="ExternalInput").ap())
    out = nc.dram_tensor("out_0", inputs["x"].shape, _mybir.dt.float32, kind="ExternalOutput").ap()
    graph_layers(nc, *args, out)
    r = _run(nc, [arrays], core_ids=[0])
    return r.results[0]["out_0"]
```

```python
import concourse.bass as bass
from concourse import mybir
from contextlib import ExitStack
from math import exp


F32 = mybir.dt.float32
F16 = mybir.dt.float16
F8 = mybir.dt.float8e5
I32 = mybir.dt.int32
U8 = mybir.dt.uint8
U16 = mybir.dt.uint16
ALU = mybir.AluOpType
ACT = mybir.ActivationFunctionType
AX = mybir.AxisListType
RMAX = bass.bass_isa.ReduceOp.max

P = 128
BW = 2048
BANK = 512
SLOTS = 4
QR = 4
CAP = 80.0
EPS = 1e-5
CODE_SCALE = 40.0
CODE_BIAS = 0.4054651 - CODE_SCALE
BIT_GT0 = 5
BIT_EQ1 = 1
BIT_2_M7 = 13
MR = 2
PLACES = {
    "attention": {"project_1": 0, "project_2": 3, "project_3": 6, "residual_1": 4, "residual_2": 7,
                  "residual_3": 10, "spread_mean": 11, "take_mean": 14, "means_0": 16, "deviations_0": 18,
                  "scales_0": 22, "normalize_0": 23, "store": 27, "finish_0": 28, "split": 30},
    "mask": {"project_1": 0, "project_2": 2, "project_3": 4, "residual_1": 4, "residual_2": 6,
             "residual_3": 8, "spread_mean": 8, "take_mean": 9, "means_0": 10, "deviations_0": 11,
             "scales_0": 14, "normalize_0": 14, "times_gamma": 16, "plus_beta": 17, "plus_x": 18,
             "means_1": 18, "deviations_1": 18, "scales_1": 21, "normalize_1": 21, "put": 14, "s2": 16,
             "turn": 14, "turned": 17, "s1_rows": 18, "s1_stored": 19, "finish_0": 17, "finish_1": 23,
             "split": 23},
    "tail": {"put": 0, "turn": 0, "turned": 4, "s1_rows": 4, "s1_stored": 8, "finish_0": 6},
    "mean_0": {"mean": 25, "mean_copied": 29},
    "mean_1": {"column": 17, "column_copied": 22, "mean": 19, "mean_copied": 23},
    "mean_3": {"column": 10, "column_copied": 15, "mean": 14, "mean_copied": 19},
}
H_APART = 5
PLACES_OF_TURN = {"attention": QR * SLOTS, "mask": QR * SLOTS // 2}
GT = 3
EB = 3
PROJECTIONS = 3
PARTS = 4
SPLIT = 4096.0


def graph_layers(nc, x, x_t, adj, w0, w0_t, a0, w1, gamma, beta, w2_t, b2, w3, w3_t, a3, b3, out):
    N, D = x.shape
    NT = N // P
    NB = N // BW
    BT = BW // P
    NQ = NT // SLOTS
    TURNS = NQ // QR
    BK = BW // BANK
    NG = -(-BT // GT)

    with ExitStack() as ctx:
        def sb(name, shape, dt):
            return ctx.enter_context(nc.sbuf_tensor(name, shape, dt))

        def sem(name):
            return ctx.enter_context(nc.semaphore(name))

        code_dram = nc.dram_tensor("code_dram", [NB * NT, P, BW], U8, kind="Internal").ap()
        code_quads = code_dram.rearrange("(n s) p w -> n p s w", s=SLOTS)

        x_in = sb("x_in", [P, NT, D], F32)
        x_cur = sb("x_cur", [P, NT, D], F32)
        w_row = sb("w_row", [P, N], F32)
        parts = {layer: ap.bitcast(F16).rearrange("p (b h t d) -> p b h t d", b=NB, h=2, t=BT)
                 for layer, ap in ((1, w_row[:, :]), (2, x_in[:, :, :].rearrange("p t d -> p (t d)")))}
        adj_sb = sb("adj_sb", [P, SLOTS, BW], I32)
        prob = sb("prob", [P, SLOTS, BW], F32)
        code = sb("code", [P, SLOTS, BW], U8)
        code_f8 = code[:, :, :].bitcast(F8)
        quads = adj_sb[:, :, :].rearrange("p s w -> p (s w)")
        quad_u8 = quads.bitcast(U8).rearrange("p (c s w) -> p c s w", c=QR, s=SLOTS)
        mask_u16 = prob[:, :, :].rearrange("p s w -> p (s w)").bitcast(U16).rearrange(
            "p (m s h w) -> p m s h w", m=MR, s=SLOTS, h=2)
        mask = prob[:, :, :].rearrange("p s w -> p (s w)").bitcast(F16).rearrange(
            "p (m s w) -> p m s w", m=MR, s=SLOTS)
        quad_u16 = quads.bitcast(U16).rearrange("p (c s w) -> p c s w", c=QR, s=SLOTS)
        sums_t = sb("sums_t", [P, BW], F32)
        res = sb("res", [P, BT, D], F32)
        sq = sb("sq", [P, BW], F32)
        sq3 = sq[:, :].rearrange("p (t d) -> p t d", d=D)
        x_t_sb = [prob[:, 3, :], res[:, :, :].rearrange("p t d -> p (t d)"), sq[:, :], sums_t[:, :]]
        s1_wide = {layer: sb(f"s1_wide{layer}", [P, P], F32) for layer in (0, 3)}
        xs = sb("xs", [P, SLOTS, D], F32)
        ident = sb("ident", [P, P], F32)
        ones = sb("ones", [P, P], F32)
        s2_row = sb("s2_row", [P, D], F32)
        eps_c = sb("eps_c", [P, 1], F32)
        minus_1 = sb("minus_1", [P, 1], F32)
        code_bias = sb("code_bias", [P, 1], F32)
        fold_t = sb("fold_t", [P, P], F32)
        proj = [sb(f"proj{n}", [P, D + 1], F32) for n in range(4)]
        w_raw = sb("w_raw", [P, 4, D], F32)
        w_tr = [prob[:, 2, n * D:(n + 1) * D] for n in range(2)]
        gamma_b = sb("gamma_b", [P, D], F32)
        beta_b = sb("beta_b", [P, D], F32)
        a_cols = sb("a_cols", [P, 4], F32)
        b3_col = sb("b3_col", [P, 1], F32)
        b2_row = sb("b2_row", [1, D], F32)
        b3_wide = prob[:, 2, 2 * D:3 * D]
        a2_wide = [prob[:, 2, n * D:(n + 1) * D] for n in (3, 4)]
        s2_row0 = prob[:, 2, 5 * D:6 * D]
        x_s2 = prob[:, 0:2, :].rearrange("p s (t d) -> p (s t) d", d=D)
        b3_b = sb("b3_b", [P, D], F32)
        sv0 = sb("sv0", [P, 2], F32)
        c3 = sb("c3", [P, 1], F32)
        s_nat = sb("s_nat", [P, NT, 2], F32)
        x_part = sb("x_part", [P, NB, D], F32)
        mean_b = sb("mean_b", [P, D], F32)
        t_wide = fold_t[:, :]
        s_max = sb("s_max", [P, 2], F32)
        w_bias = sb("w_bias", [P, 1], F32)
        r_nat = sb("r_nat", [P, NT], F32)
        v_nat = sb("v_nat", [P, NT], F32)
        v_mean = sb("v_mean", [P, NT], F32)
        den = sb("den", [P, 4, BT], F32)
        s2_rel = den[:, :, :].rearrange("p a t -> p (a t)")
        stat = sb("stat", [P, 5, BT], F32)

        acc = ctx.enter_context(nc.psum_tensor("acc", [P, BK, BANK], F32))
        epi = [ctx.enter_context(nc.psum_tensor(f"epi{n}", [P, BANK], F32)) for n in range(EB)]
        small = ctx.enter_context(nc.psum_tensor("small", [P, BANK], F32))
        banks = [e[:, :] for e in epi] + [small[:, :]]
        SNAT = small[:, 0:NT].rearrange("p (t c) -> p t c", c=2)
        MEAN = small[:, 128:256]
        COL = small[:, 256:257]

        weights_in = sem("weights_in")
        x_loaded = [sem(f"x_loaded{half}") for half in range(2)]
        x_t_in = [sem(f"x_t_in{n}") for n in range(4)]
        consts_ready = sem("consts_ready")
        fold_ready = sem("fold_ready")
        fold_products = sem("fold_products")
        s1_wide_ready = sem("s1_wide_ready")
        weights_ready = sem("weights_ready")
        h_ready = sem("h_ready")
        h_used = sem("h_used")
        s0_ready = sem("s0_ready")
        s0_used = sem("s0_used")
        dve_chain = sem("dve_chain")
        adj_in = [sem(f"adj_in{k}") for k in range(SLOTS)]
        adj_coded = sem("adj_coded")
        quad_used = sem("quad_used")
        code_stored = [sem(f"code_stored{k}") for k in range(SLOTS)]
        out_stored = sem("out_stored")

        named = {}

        def of(layer, name):
            key = f"l{layer}_{name}"
            if key not in named:
                named[key] = sem(key)
            return named[key]

        LAYERS = (0, 1, 2, 3)
        ATTENTION = {0: 0.01, 3: 0.2}
        MEAN_ROWS = (0, 1, 3)
        LAYER_NORMS = {0: 1, 1: 2, 2: 1, 3: 1}

        def is_at(index, n):
            return isinstance(index, int) and index == n

        def kind(layer):
            return "attention" if layer in ATTENTION else "mask"

        def nothing():
            pass

        NOTHING = [nothing] * (QR * SLOTS)

        def at_places(layer, items):
            apart = 1 if layer in ATTENTION else 0
            items = [(place + n * apart, part) for place, piece in items
                     for n, part in enumerate(piece if isinstance(piece, list) else [piece])]
            per_turn = PLACES_OF_TURN[kind(layer)]
            late = [[] for _ in range(max([place for place, _ in items] + [0]) // per_turn * per_turn + per_turn)]
            for place, piece in items:
                late[place].append(piece)
            return [(lambda those=those: [piece() for piece in those]) for those in late]

        def items(where, pieces):
            return [(PLACES[where][name], piece) for name, piece in pieces.items() if name in PLACES[where]]

        def placed(layer, pieces):
            return at_places(layer, items(kind(layer), pieces))

        def in_parts(piece):
            return [lambda n=n: piece(range(n * BT // PARTS, (n + 1) * BT // PARTS)) for n in range(PARTS)]

        def groups_of(part):
            return range(part * NG // PROJECTIONS, (part + 1) * NG // PROJECTIONS)

        def tiles_of(part):
            return range(groups_of(part)[0] * GT, min((groups_of(part)[-1] + 1) * GT, BT))

        def by_projection(piece):
            return [lambda part=part: piece(part) for part in range(PROJECTIONS)]

        def run(pieces, but=()):
            fore = [[f"project_{part + 1}", f"residual_{part + 1}", "spread_mean"] for part in range(PROJECTIONS)] + [[]]
            behind = ["take_mean", "means_0", "deviations_0"]
            for part, names in enumerate(fore):
                for name in names:
                    if name in pieces:
                        pieces[name][part]() if isinstance(pieces[name], list) else pieces[name]()
                for name in behind:
                    if part and name in pieces:
                        pieces[name][part - 1]()
            done = behind + [name for names in fore for name in names]
            for name, piece in pieces.items():
                if name not in but and name not in done:
                    for part in piece if isinstance(piece, list) else [piece]:
                        part()

        def blocks(eng, layer, quad, first_late, pieces, peel_last=False):
            per_turn = PLACES_OF_TURN[kind(layer)]
            per_quad = per_turn // QR

            def turn_of(ib, turn, late):
                for c in range(QR):
                    quad(ib, turn, c, late[c * per_quad:(c + 1) * per_quad])

            def one(ib, late):
                straight = len(late) // per_turn
                for turn in range(straight):
                    turn_of(ib, turn, late[turn * per_turn:(turn + 1) * per_turn])
                turn_ends = max(TURNS - 1 if peel_last else TURNS, straight)
                if turn_ends - straight > 1:
                    with eng.Fori(straight, turn_ends) as turn:
                        turn_of(ib, turn, NOTHING)
                else:
                    for turn in range(straight, turn_ends):
                        turn_of(ib, turn, NOTHING)
                for turn in range(turn_ends, TURNS):
                    turn_of(ib, turn, NOTHING)

            one(0, first_late)
            with eng.Fori(1, NB) as ib:
                one(ib, placed(layer, pieces(ib - 1)))

        block = ctx.enter_context(nc.Block())

        @block.sync
        def _(sp):
            for dst, src in ((w_raw[:, 0, :], w0), (w_tr[0], w0_t), (w_raw[:, 1, :], w1), (w_raw[:, 2, :], w2_t),
                             (w_raw[:, 3, :], w3), (w_tr[1], w3_t), (a_cols[:, 0:2], a0), (a_cols[:, 2:4], a3),
                             (b3_col[:, :], b3.rearrange("(d a) -> d a", a=1)),
                             (b2_row[:, :], b2.rearrange("(a d) -> a d", a=1)),
                             (b3_b[:, :], b3.partition_broadcast(P)),
                             (gamma_b[:, :], gamma.partition_broadcast(P)),
                             (beta_b[:, :], beta.partition_broadcast(P))):
                sp.dma_start(dst, src).then_inc(weights_in, 16)
            def load_x_t(n):
                sp.dma_start(x_t_sb[n], x_t[:, n * BW:(n + 1) * BW]).then_inc(x_t_in[n], 16)

            def load_x(half):
                tiles = slice(half * NT // 2, (half + 1) * NT // 2)
                sp.dma_start(x_in[:, tiles, :], x.rearrange("(t p) d -> p t d", p=P)[:, tiles, :])\
                    .then_inc(x_loaded[half], 16)

            load_x_t(0)
            load_x(1)
            load_x_t(1)
            load_x(0)
            for k in range(SLOTS):
                sp.dma_start(adj_sb[:, k, :], adj[k]).then_inc(adj_in[k], 16)
            for n in range(2, NB):
                load_x_t(n)
            with sp.Fori(1, NB * NQ) as q:
                for k in range(SLOTS):
                    sp.wait_ge(of(0, "prob_ready"), (q - 1) * SLOTS + (k + 1))
                    sp.wait_ge(adj_coded, (q - 1) * SLOTS + (k + 1))
                    sp.dma_start(adj_sb[:, k, :], adj[q * SLOTS + k]).then_inc(adj_in[k], 16)
            for layer in (1, 2, 3):
                for c in range(QR):
                    if layer == 1:
                        sp.wait_ge(of(0, "prob_ready"), NB * NT - SLOTS + (c + 1))
                        sp.wait_ge(adj_coded, NB * NT - SLOTS + (c + 1))
                        if c == 0:
                            for k in range(SLOTS):
                                sp.wait_ge(code_stored[k], 16 * NB * NQ)
                    else:
                        sp.wait_ge(of(layer - 1, "mask_ready"), NB * NQ - QR + (c + 1))
                    sp.dma_start(quad_u8[:, c, :, :], code_quads[c]).then_inc(of(layer, f"code_in{c}"), 16)
                if layer == 1:
                    for k in range(SLOTS):
                        sp.wait_ge(code_stored[k], 16 * NB * NQ + 16)
                with sp.Fori(1, NB * TURNS) as turn:
                    for c in range(QR):
                        if layer in ATTENTION:
                            sp.wait_ge(of(layer, "prob_ready"), (turn - 1) * (QR * SLOTS) + (c + 1) * SLOTS)
                        else:
                            sp.wait_ge(of(layer, "mask_ready"), (turn - 1) * QR + (c + 1))
                        sp.dma_start(quad_u8[:, c, :, :], code_quads[turn * QR + c])\
                            .then_inc(of(layer, f"code_in{c}"), 16)

        @block.gpsimd
        def _(pool):
            nc.gpsimd.memset(ones[:, :], 1.0).then_inc(consts_ready, 1)
            nc.gpsimd.memset(eps_c[:, :], EPS).then_inc(consts_ready, 1)
            nc.gpsimd.memset(minus_1[:, :], -1.0).then_inc(consts_ready, 1)
            nc.gpsimd.memset(code_bias[:, :], CODE_BIAS).then_inc(consts_ready, 1)
            nc.gpsimd.memset(ident[:, :], 0.0).then_inc(consts_ready, 1)
            pool.wait_ge(consts_ready, 5)
            nc.gpsimd.affine_select(out=ident[:, :], in_=ident[:, :], compare_op=ALU.not_equal, fill=1.0, base=0,
                                    pattern=[[-1, P]], channel_multiplier=1).then_inc(consts_ready, 1)
            for layer in ATTENTION:
                pool.wait_ge(of(layer, "smax_ready"), 1)
                nc.gpsimd.partition_all_reduce(s_max[:, 1:2], s_max[:, 0:1], P, RMAX).then_inc(of(layer, "s_all"), 1)

        @block.scalar
        def _(act):
            def exps(layer):
                al = ATTENTION[layer]
                if layer:
                    nc.scalar.activation(v_nat[:, 0:1], minus_1[:, 0:1], ACT.Exp).then_inc(of(3, "table_in"), 1)
                    act.wait_ge(of(3, "table_in"), 1)
                act.wait_ge(of(layer, "logs_ready"), 1)
                nc.scalar.activation(r_nat[:, :], s2_rel, ACT.Exp, scale=1.0 - al)\
                    .then_inc(of(layer, "exps_ready"), 1)
                nc.scalar.activation(v_nat[:, :], s2_rel, ACT.Exp, scale=al)\
                    .then_inc(of(layer, "exps_ready"), 1)

            def first_rows(g):
                act.wait_ge(of(0, "row_ready"), g + 1)
                src = acc[:, g, :] if g < BK else small[:, :]
                nc.scalar.activation(w_row[:, g * BANK:(g + 1) * BANK], src, ACT.Exp, scale=1.0 - ATTENTION[0],
                                     bias=w_bias[:, 0:1]).then_inc(of(0, "row_exps"), 1)

            def last_rows(ib):
                act.wait_ge(of(3, "s1_copied"), (ib + 2) * BK)
                nc.scalar.activation(w_row[:, ib * BW:(ib + 1) * BW], w_row[:, ib * BW:(ib + 1) * BW], ACT.Exp,
                                     scale=1.0 - ATTENTION[3], bias=w_bias[:, 0:1]).then_inc(of(3, "row_exps"), BK)

            def stationary(layer, j, k, count):
                act.wait_ge(of(layer, "prob_used"), count)
                src = x_in if layer == 0 else x_cur
                nc.scalar.activation(xs[:, k, 1:D], src[:, j, 1:D], ACT.Identity, scale=v_nat[:, j],
                                     bias=v_mean[:, j]).then_inc(of(layer, "xs_ready"), 1)
                nc.scalar.copy(xs[:, k, 0:1], v_nat[:, j]).then_inc(of(layer, "xs_ready"), 1)

            def take_sums(layer, ib):
                if layer in ATTENTION:
                    act.wait_ge(of(layer, "prob_used"), ib * NT + (NT + SLOTS))
                else:
                    act.wait_ge(quad_used, ((layer - 1) * NB + ib) * NQ + (NQ + MR))
                for b in range(BK):
                    nc.scalar.copy(sums_t[:, b * BANK:(b + 1) * BANK], acc[:, b, :])\
                        .then_inc(of(layer, "sums_ready"), 1)

            def pieces(layer, ib):
                norms = LAYER_NORMS[layer]

                def deviations(n, part):
                    act.wait_ge(of(layer, "means_ready"), (ib * norms + n) * PROJECTIONS + (part + 1))
                    tiles = tiles_of(part)
                    for t in tiles:
                        ins = nc.scalar.activation(sq3[:, t, :], res[:, t, :], ACT.Square, bias=stat[:, 0, t:t + 1],
                                                   accum_out=stat[:, 1, t:t + 1])
                    if tiles[-1] < BT - 1:
                        return
                    ins.then_inc(of(layer, "squared"), 1)
                    act.wait_ge(of(layer, "squared"), ib * norms + (n + 1))
                    nc.scalar.activation(stat[:, 2, :], stat[:, 1, :], ACT.Sqrt, scale=1.0 / D, bias=eps_c[:, 0:1])\
                        .then_inc(of(layer, "std_ready"), 1)

                def normalize(tiles):
                    act.wait_ge(of(layer, "scales_ready"), ib + 1)
                    for t in tiles:
                        ins = nc.scalar.activation(x_cur[:, bass.ds(ib * BT + t, 1), :].rearrange("p a d -> p (a d)"),
                                                   res[:, t, :], ACT.Identity, scale=stat[:, 3, t:t + 1],
                                                   bias=stat[:, 4, t:t + 1])
                    if tiles[-1] == BT - 1:
                        ins.then_inc(of(layer, "x_stored"), 1)

                def put_result():
                    act.wait_ge(of(layer, "normed"), ib + 1)
                    nc.scalar.copy(x_cur[:, bass.ds(ib * BT, BT), :], res[:, :, :]).then_inc(of(layer, "x_stored"), 1)

                def store():
                    act.wait_ge(of(layer, "normed"), ib + 1)
                    act.dma_start(out.rearrange("(b t p) d -> b p t d", p=P, t=BT)[ib], res[:, :, :])\
                        .then_inc(out_stored, 16)

                def turned():
                    act.wait_ge(of(2, "s2_summed"), ib + 1)
                    for g in range(BK):
                        act.wait_ge(of(layer, "tr_ready"), ib * BK + (g + 1))
                        nc.scalar.copy(sq[:, g * BANK:(g + 1) * BANK], banks[g])\
                            .then_inc(of(layer, "tr_copied"), 1)

                def s1_stored():
                    for g in range(BK):
                        act.wait_ge(of(3, "s1_ready"), ib * BK + (g + 1))
                        nc.scalar.copy(w_row[:, bass.ds(ib * BW + g * BANK, BANK)], banks[g])\
                            .then_inc(of(3, "s1_copied"), 1)

                def split():
                    act.wait_ge(of(layer, "x_stored"), ib + 2)
                    nc.scalar.activation(parts[layer + 1][:, bass.ds(ib, 1), 0, :, 1:D].rearrange("p b t d -> p (b t) d"),
                                         x_cur[:, bass.ds(ib * BT, BT), 1:D],
                                         ACT.Copy, scale=SPLIT).then_inc(of(layer + 1, "hi_ready"), 1)

                def spread_mean(part):
                    act.wait_ge(of(layer, "proj_read"), ib * NG + (groups_of(part)[-1] + 1 + EB))
                    for t in tiles_of(part):
                        ins = nc.scalar.activation(sq3[:, t, :], mean_b[:, :], ACT.Copy, scale=den[:, 1, t:t + 1])
                    ins.then_inc(of(layer, "mean_spread"), 1)

                late = {"spread_mean": by_projection(spread_mean)} if layer in MEAN_ROWS else {}
                for n in range(norms):
                    late[f"deviations_{n}"] = by_projection(lambda part, n=n: deviations(n, part))
                    if layer == 0:
                        late[f"normalize_{n}"] = in_parts(normalize)
                if layer == 2:
                    late.update(put=put_result, turned=turned, s1_stored=s1_stored)
                else:
                    late.update({"store": store} if layer == 3 else {"split": split})
                return late

            def attention_quad(layer, ib, turn, c, late):
                q = turn * QR + c
                for k in range(SLOTS):
                    step = ib * NT + q * SLOTS + k
                    j = bass.ds(q * SLOTS + k, 1)
                    if layer == 0:
                        act.wait_ge(adj_in[k], (ib * NQ + q) * 16 + 16)
                        act.wait_ge(code_stored[k], (ib * NQ + q) * 16 + 16)
                    stationary(layer, j, k, step + 1)
                    if layer == 0:
                        nc.scalar.activation(code_f8[:, k, :].rearrange("p (a h) -> p h a", h=2),
                                             adj_sb[:, k, :].rearrange("p (h a) -> p h a", h=2), ACT.Exp,
                                             scale=CODE_SCALE, bias=code_bias[:, 0:1], saturate=False)\
                            .then_inc(adj_coded, 1)
                        act.wait_ge(adj_coded, step + 1)
                        act.dma_start(code_dram[step], code[:, k, :]).then_inc(code_stored[k], 16)
                    else:
                        if k == 0 and c == 0 and is_at(turn, 0) and is_at(ib, 0):
                            act.wait_ge(of(3, "row_capped"), 1)
                        elif k == 0 and c == 0 and is_at(turn, 0):
                            act.wait_ge(of(3, "row_capped"), ib + 1)
                        nc.scalar.activation(prob[:, k, :], w_row[:, bass.ds(ib * BW, BW)], ACT.Relu,
                                             scale=r_nat[:, j], bias=minus_1[:, 0:1]).then_inc(of(3, "t_ready"), 1)
                    if k == 1 and c == 0 and is_at(turn, 0) and not is_at(ib, 0):
                        take_sums(layer, ib - 1)
                    late[k]()

            def mask_quad(layer, ib, turn, c, late):
                if c == 0 and is_at(turn, 0) and not is_at(ib, 0):
                    take_sums(layer, ib - 1)
                late[0]()
                late[1]()

            act.wait_ge(consts_ready, 6)
            for k in range(SLOTS):
                act.sem_inc(code_stored[k], 16)
            for layer in LAYERS:
                if layer in ATTENTION:
                    exps(layer)
                    if layer == 0:
                        for g in range(BK):
                            first_rows(g)
                        late = at_places(0, [((g - BK + 1) * H_APART, lambda g=g: first_rows(g))
                                             for g in range(BK, NB * BK)])
                    else:
                        last_rows(0)
                        late = at_places(3, items("tail", last_of_2) + [
                            (1, lambda: act.wait_ge(of(2, "x_stored"), NB + 1))] + [
                            (4 * ib + 1, lambda ib=ib: last_rows(ib)) for ib in range(1, NB)])
                    act.wait_ge(of(layer, "bias_ready"), 1)
                    blocks(act, layer, lambda ib, turn, c, late: attention_quad(layer, ib, turn, c, late), late,
                           lambda ib: pieces(layer, ib))
                else:
                    take_sums(layer - 1, NB - 1)
                    blocks(act, layer, lambda ib, turn, c, late: mask_quad(layer, ib, turn, c, late),
                           placed(layer, pieces(layer - 1, NB - 1)), lambda ib: pieces(layer, ib))
                if layer >= 2:
                    take_sums(layer, NB - 1)
                    last_of_2 = pieces(layer, NB - 1)
                    run(last_of_2, but=PLACES["tail"])
            act.wait_ge(out_stored, 16 * NB + 16)

        @block.vector
        def _(dve):
            count = [0]

            def link(ins):
                count[0] += 1
                ins.then_inc(dve_chain, 1)
                dve.wait_ge(dve_chain, count[0])

            def prepare_weights():
                dve.wait_ge(consts_ready, 6)
                nc.vector.tensor_copy(fold_t[:, :], ident[:, :]).then_inc(fold_ready, 1)
                nc.vector.tensor_copy(proj[0][:, 0:D], ident[:, :]).then_inc(fold_ready, 1)
                dve.wait_ge(fold_ready, 2)
                nc.vector.memset(fold_t[0:1, :], -1.0).then_inc(fold_ready, 1)
                nc.vector.memset(proj[0][:, 0:1], -1.0).then_inc(fold_ready, 1)
                dve.wait_ge(fold_ready, 4)
                nc.vector.memset(fold_t[0:1, 0:1], 0.0).then_inc(fold_ready, 1)
                nc.vector.memset(proj[0][0:1, 0:1], 0.0).then_inc(fold_ready, 1)
                for n in range(4):
                    link(nc.vector.tensor_copy(proj[n][:, D:D + 1], ident[:, 0:1]))
                dve.wait_ge(weights_in, 16 * 13)
                nc.vector.tensor_scalar(b3_wide, ones[:, :], b3_col[:, 0:1], None, ALU.mult).then_inc(fold_ready, 1)
                for n in range(2):
                    nc.vector.tensor_scalar(a2_wide[n], ones[:, :], a_cols[:, 2 * n + 1:2 * n + 2], None, ALU.mult)\
                        .then_inc(fold_ready, 1)
                dve.wait_ge(fold_products, 1)
                link(nc.vector.tensor_scalar(proj[1][:, 0:D], epi[0][:, 0:D], 1.0 / SPLIT, None, ALU.mult))
                link(nc.vector.tensor_scalar(proj[2][:, 0:D], epi[0][:, D:2 * D], 1.0 / SPLIT, None, ALU.mult))
                link(nc.vector.tensor_copy(proj[3][:, 0:D], epi[0][:, 2 * D:3 * D]))
                link(nc.vector.tensor_copy(proj[2][0:1, 0:D], b2_row[:, :]))
                link(nc.vector.tensor_copy(proj[3][0:1, 0:D], b3_b[0:1, :]))
                nc.vector.tensor_scalar(s1_wide[0][:, :], ones[:, :], epi[1][:, 0:1], None, ALU.mult)\
                    .then_inc(s1_wide_ready, 1)
                link(nc.vector.memset(sv0[:, 1:2], 1.0 / D))
                link(nc.vector.tensor_copy(sv0[:, 0:1], epi[1][:, 1:2]))
                link(nc.vector.tensor_copy(s2_row[:, :], epi[1][:, D:2 * D]))
                link(nc.vector.tensor_copy(s2_row0, epi[1][:, 2 * D:3 * D]))
                nc.vector.tensor_scalar(s1_wide[3][:, :], ones[:, :], epi[1][:, 2:3], None, ALU.mult)\
                    .then_inc(s1_wide_ready, 1)
                nc.vector.tensor_reduce(c3[:, :], epi[1][:, 4:6], AX.X, ALU.add).then_inc(weights_ready, 1)

            def first_s():
                half = NT // 2
                dve.wait_ge(x_loaded[1], 16)
                link(nc.vector.tensor_tensor(x_s2, x_in[:, half:, :], s2_row0.unsqueeze(1).to_broadcast([P, half, D]),
                                             ALU.mult))
                nc.vector.tensor_reduce(s_nat[:, half:, 0:1].rearrange("p t a -> p (t a)"), x_s2, AX.X, ALU.add)
                link(nc.vector.tensor_reduce(s_nat[:, half:, 1:2].rearrange("p t a -> p (t a)"), x_in[:, half:, :], AX.X,
                                             ALU.add))
                link(nc.vector.tensor_scalar(s_nat[:, half:, 1:2], s_nat[:, half:, 1:2], 1.0 / D, None, ALU.mult))
                dve.wait_ge(s0_ready, 1)
                nc.vector.tensor_copy(s_nat[:, 0:half, :], SNAT).then_inc(s0_used, 1)

            def add_h(n):
                if n == 0:
                    dve.wait_ge(x_loaded[0], 16)
                dve.wait_ge(h_ready, n + 1)
                nc.vector.tensor_tensor(x_cur[:, 4 * n:4 * n + 4, :], epi[n % EB][:, :].rearrange("p (t d) -> p t d", d=D),
                                        x_in[:, 4 * n:4 * n + 4, :], ALU.add).then_inc(h_used, 1)

            def sum_x(ib):
                nc.vector.tensor_reduce(x_part[:, ib, :], x_in[:, ib * BT:(ib + 1) * BT, :].rearrange("p t d -> p d t"),
                                        AX.X, ALU.add).then_inc(of(0, "sum_ready"), 1)

            def mean_pieces(layer):
                def column_copied():
                    dve.wait_ge(of(layer, "col_ready"), 1)
                    nc.vector.tensor_scalar(t_wide, ones[:, :], COL, 1.0 / N, ALU.mult, ALU.mult)\
                        .then_inc(of(layer, "col_copied"), 1)

                def mean_copied():
                    dve.wait_ge(of(layer, "mean_product"), 1)
                    if layer == 3:
                        ins = nc.vector.tensor_tensor(mean_b[:, :], MEAN, b3_b[:, :], ALU.add)
                    elif layer == 1:
                        ins = nc.vector.tensor_copy(mean_b[:, :], MEAN)
                    else:
                        ins = nc.vector.tensor_scalar(mean_b[:, :], MEAN, 1.0 / N, None, ALU.mult)
                    ins.then_inc(of(layer, "mean_ready"), 1)
                    dve.wait_ge(of(layer, "mean_ready"), 1)

                return {"column_copied": column_copied, "mean_copied": mean_copied} if layer \
                    else {"mean_copied": mean_copied}

            def cap_row(layer, ib):
                dve.wait_ge(of(layer, "row_exps"), (ib + 1) * BK)
                nc.vector.tensor_scalar(w_row[:, ib * BW:(ib + 1) * BW], w_row[:, ib * BW:(ib + 1) * BW], exp(CAP), None,
                                        ALU.min).then_inc(of(layer, "row_capped"), 1)

            def attention_rows(layer):
                al = ATTENTION[layer]
                if layer == 0:
                    dve.wait_ge(s0_used, 1)
                else:
                    dve.wait_ge(of(2, "s2_summed"), NB)
                nc.vector.tensor_reduce(s_max[:, 0:1], s_nat[:, :, 0], AX.X, ALU.max)\
                    .then_inc(of(layer, "smax_ready"), 1)
                if layer == 0:
                    for n in range(BK):
                        add_h(n)
                dve.wait_ge(of(layer, "s_all"), 1)
                if layer == 0:
                    nc.vector.tensor_scalar(w_bias[:, :], s_max[:, 1:2], 1.0 - al, None, ALU.mult)
                else:
                    nc.vector.tensor_scalar(w_bias[:, :], s_max[:, 1:2], c3[:, 0:1], 1.0 - al, ALU.add, ALU.mult)
                nc.vector.tensor_scalar(s2_rel, s_nat[:, :, 0], s_max[:, 1:2], None, ALU.subtract)\
                    .then_inc(of(layer, "logs_ready"), 1)
                dve.wait_ge(of(layer, "exps_ready"), 2)
                if layer == 0:
                    nc.vector.scalar_tensor_tensor(v_mean[:, :], v_nat[:, :], -1.0, s_nat[:, :, 1], ALU.mult,
                                                   ALU.mult).then_inc(of(layer, "bias_ready"), 1)
                else:
                    nc.vector.memset(v_mean[:, :], 0.0).then_inc(of(layer, "bias_ready"), 1)
                cap_row(layer, 0)

            CHAIN = {0: 22, 1: 31, 2: 15, 3: 23}

            def pieces(layer, ib):
                done = [0]
                mean_rows = layer in MEAN_ROWS
                norms = LAYER_NORMS[layer]

                def mark(ins):
                    done[0] += 1
                    ins.then_inc(of(layer, "chain"), 1)

                def tie(ins):
                    mark(ins)
                    dve.wait_ge(of(layer, "chain"), ib * CHAIN[layer] + done[0])

                def residual(groups):
                    t0, t1 = groups[0] * GT, min(groups[-1] * GT + GT, BT)
                    for g in groups:
                        dve.wait_ge(of(layer, "proj_ready"), ib * NG + (g + 1))
                        n = min(GT, BT - g * GT)
                        mark(nc.vector.tensor_copy(
                            den[:, 0, g * GT:g * GT + n],
                            epi[g % EB][:, 0:n * (D + 1)].rearrange("p (k c) -> p k c", c=D + 1)[:, :, D]))
                    dve.wait_ge(of(layer, "chain"), ib * CHAIN[layer] + done[0])
                    full = 0
                    if mean_rows:
                        tie(nc.vector.tensor_scalar(den[:, 1, t0:t1], den[:, 0, t0:t1], 0.0, None, ALU.is_equal))
                        tie(nc.vector.tensor_tensor(den[:, 2, t0:t1], den[:, 0, t0:t1], den[:, 1, t0:t1], ALU.add))
                        full = 2
                    tie(nc.vector.reciprocal(den[:, 3, t0:t1], den[:, full, t0:t1]))
                    if groups[0] == 0:
                        if layer == 3:
                            dve.wait_ge(out_stored, ib * 16 + 16)
                        else:
                            dve.wait_ge(of(layer, "x_stored"), ib + 1)
                    for g in groups:
                        for t in range(g * GT, min(g * GT + GT, BT)):
                            k = t - g * GT
                            src = epi[g % EB][:, k * (D + 1):k * (D + 1) + D]
                            if layer == 1:
                                ins = nc.vector.tensor_scalar(res[:, t, :], src, den[:, 3, t:t + 1], None, ALU.mult)
                            else:
                                ins = nc.vector.scalar_tensor_tensor(
                                    res[:, t, :], src, den[:, 3, t:t + 1],
                                    x_cur[:, bass.ds(ib * BT + t, 1), :].rearrange("p a d -> p (a d)"), ALU.mult, ALU.add)
                        ins.then_inc(of(layer, "proj_read"), 1)

                def take_mean(part):
                    tiles = slice(tiles_of(part)[0], tiles_of(part)[-1] + 1)
                    dve.wait_ge(of(layer, "proj_read"), ib * NG + (groups_of(part)[-1] + 1 + EB))
                    dve.wait_ge(of(layer, "mean_spread"), ib * PROJECTIONS + (part + 1))
                    tie(nc.vector.tensor_tensor(res[:, tiles, :], res[:, tiles, :], sq3[:, tiles, :], ALU.add))

                def means(n, part):
                    tiles = slice(tiles_of(part)[0], tiles_of(part)[-1] + 1)
                    if n == 0:
                        dve.wait_ge(of(layer, "proj_read"), ib * NG + (groups_of(part)[-1] + 1 + EB))
                    tie(nc.vector.tensor_reduce(stat[:, 4, tiles], res[:, tiles, :], AX.X, ALU.add))
                    nc.vector.tensor_scalar(stat[:, 0, tiles], stat[:, 4, tiles], -1.0 / D, None, ALU.mult)\
                        .then_inc(of(layer, "means_ready"), 1)

                def scales(n):
                    dve.wait_ge(of(layer, "std_ready"), ib * norms + (n + 1))
                    tie(nc.vector.reciprocal(stat[:, 3, :], stat[:, 2, :]))
                    ins = nc.vector.tensor_tensor(stat[:, 4, :], stat[:, 3, :], stat[:, 0, :], ALU.mult)
                    if layer == 0:
                        ins.then_inc(of(layer, "scales_ready"), 1)
                    else:
                        tie(ins)

                def normalize(n, tiles):
                    to_x = layer == 1 and n == 1
                    for t in tiles:
                        to = x_cur[:, bass.ds(ib * BT + t, 1), :].rearrange("p a d -> p (a d)") if to_x else res[:, t, :]
                        ins = nc.vector.tensor_scalar(to, res[:, t, :], stat[:, 3, t:t + 1], stat[:, 4, t:t + 1],
                                                      ALU.mult, ALU.add)
                    if tiles[-1] == BT - 1:
                        ins.then_inc(of(layer, "x_stored" if to_x else "normed"), 1)

                def times_gamma():
                    dve.wait_ge(of(layer, "normed"), ib + 1)
                    tie(nc.vector.tensor_tensor(res[:, :, :], res[:, :, :],
                                                gamma_b[:, :].unsqueeze(1).to_broadcast([P, BT, D]), ALU.mult))

                def plus_beta():
                    tie(nc.vector.tensor_tensor(res[:, :, :], res[:, :, :],
                                                beta_b[:, :].unsqueeze(1).to_broadcast([P, BT, D]), ALU.add))

                def plus_x():
                    tie(nc.vector.tensor_tensor(res[:, :, :], res[:, :, :], x_cur[:, bass.ds(ib * BT, BT), :], ALU.add))

                def next_s2():
                    dve.wait_ge(of(2, "normed"), ib + 1)
                    tie(nc.vector.tensor_tensor(sq3, res[:, :, :], s2_row[:, :].unsqueeze(1).to_broadcast([P, BT, D]),
                                                ALU.mult))
                    nc.vector.tensor_reduce(s_nat[:, bass.ds(ib * BT, BT), 0:1].rearrange("p t a -> p (t a)"), sq3, AX.X,
                                            ALU.add).then_inc(of(2, "s2_summed"), 1)

                def finish():
                    if layer + 1 in MEAN_ROWS:
                        dve.wait_ge(of(layer, "x_stored"), ib + 2)
                        nc.vector.tensor_reduce(x_part[:, bass.ds(ib, 1), :].rearrange("p a d -> p (a d)"),
                                                x_cur[:, bass.ds(ib * BT, BT), :].rearrange("p t d -> p d t"),
                                                AX.X, ALU.add).then_inc(of(layer + 1, "sum_ready"), 1)
                    assert done[0] == CHAIN[layer], (layer, done[0])

                def split():
                    dve.wait_ge(of(layer + 1, "hi_ready"), ib + 1)
                    hi_lo = parts[layer + 1][:, bass.ds(ib, 1), :, :, :].rearrange("p b h t d -> p (b h) t d")
                    for h in range(2):
                        nc.vector.tensor_scalar(hi_lo[:, h, :, 0:1], ones[:, 0:BT].unsqueeze(2), 1.0 - h, None, ALU.mult)
                    nc.vector.scalar_tensor_tensor(hi_lo[:, 1, :, 1:D], x_cur[:, bass.ds(ib * BT, BT), 1:D], SPLIT,
                                                   hi_lo[:, 0, :, 1:D], ALU.mult, ALU.subtract)\
                        .then_inc(of(layer + 1, "lo_ready"), 1)

                late = {f"residual_{n + 1}": lambda n=n: residual(groups_of(n)) for n in range(PROJECTIONS)}
                if mean_rows:
                    late["take_mean"] = by_projection(take_mean)
                for n in range(norms):
                    if n == 1:
                        late.update(times_gamma=times_gamma, plus_beta=plus_beta, plus_x=plus_x)
                    late[f"means_{n}"] = by_projection(lambda part, n=n: means(n, part))
                    late[f"scales_{n}"] = lambda n=n: scales(n)
                    if layer:
                        late[f"normalize_{n}"] = in_parts(lambda tiles, n=n: normalize(n, tiles))
                if layer == 2:
                    late["s2"] = next_s2
                late[f"finish_{norms - 1}"] = finish
                if layer < 2:
                    late["split"] = split
                return late

            def adjacency_quad(ib, turn, c, late):
                q = turn * QR + c
                for pair in range(0, SLOTS, 2):
                    step = ib * NT + q * SLOTS + pair
                    for k in range(pair, pair + 2):
                        j = bass.ds(q * SLOTS + k, 1)
                        if k == 0 and c == 0 and is_at(turn, 0):
                            dve.wait_ge(of(0, "row_capped"), 1 if is_at(ib, 0) else ib + 1)
                        dve.wait_ge(of(0, "prob_used"), step + (k - pair + 1))
                        nc.vector.tensor_scalar(prob[:, k, :], w_row[:, bass.ds(ib * BW, BW)], r_nat[:, j],
                                                1.0, ALU.mult, ALU.max).then_inc(of(0, "t_ready"), 1)
                    for k in range(pair, pair + 2):
                        dve.wait_ge(of(0, "t_ready"), step + (k - pair + 1))
                        dve.wait_ge(adj_in[k], (ib * NQ + q) * 16 + 16)
                        nc.vector.scalar_tensor_tensor(prob[:, k, :], adj_sb[:, k, :], 0.0, prob[:, k, :],
                                                       ALU.is_gt, ALU.mult).then_inc(of(0, "prob_ready"), 1)
                    late[pair]()
                    late[pair + 1]()

            def codes_in(layer, ib, turn, c):
                dve.wait_ge(of(layer, f"code_in{c}"), (ib * TURNS + turn) * 16 + 16)

            def mask_quad(layer, ib, turn, c, late):
                bit = BIT_EQ1 if layer == 2 else BIT_GT0
                codes_in(layer, ib, turn, c)
                if layer == 1 and is_at(ib, 0) and is_at(turn, 0) and c < MR:
                    dve.wait_ge(of(0, "prob_used"), NB * NT + (c + 1) * (SLOTS // MR))
                dve.wait_ge(quad_used, ((layer - 1) * NB + ib) * NQ + turn * QR + (c + 1))
                nc.vector.tensor_scalar(mask_u16[:, c % MR, :, 0, :], quad_u16[:, c, :, :], 1 << bit, BIT_2_M7 - bit,
                                        ALU.bitwise_and, ALU.logical_shift_left)
                nc.vector.tensor_scalar(mask_u16[:, c % MR, :, 1, :], quad_u16[:, c, :, :], 1 << (bit + 8),
                                        BIT_2_M7 - bit - 8, ALU.bitwise_and, ALU.logical_shift_left)\
                    .then_inc(of(layer, "mask_ready"), 1)
                late[0]()
                late[1]()

            def attention_quad(ib, turn, c, late):
                q = turn * QR + c
                codes_in(3, ib, turn, c)
                nc.vector.tensor_scalar(quad_u16[:, c, :, :], quad_u16[:, c, :, :], 0x101 << BIT_GT0, None,
                                        ALU.bitwise_and).then_inc(of(3, "mask_ready"), 1)
                dve.wait_ge(of(3, "mask_ready"), ib * NQ + q + 1)
                for k in range(SLOTS):
                    dve.wait_ge(of(3, "t_ready"), ib * NT + q * SLOTS + (k + 1))
                    halves = prob[:, k, :].rearrange("p (h a) -> p h a", h=2)
                    nc.vector.scalar_tensor_tensor(halves, halves, 1.0,
                                                   quad_u8[:, c, k, :].rearrange("p (a h) -> p h a", h=2),
                                                   ALU.add, ALU.mult).then_inc(of(3, "prob_ready"), 1)
                    late[k]()

            prepare_weights()
            first_s()
            for layer in LAYERS:
                if layer == 3:
                    dve.sem_inc(out_stored, 16)
                else:
                    dve.sem_inc(of(layer, "x_stored"), 1)
                means_late = items(f"mean_{layer}", mean_pieces(layer)) if layer in MEAN_ROWS else []
                if layer in ATTENTION:
                    attention_rows(layer)
                    late = [((BK * H_APART * ib if layer == 0 else 5 * ib) + 1, lambda ib=ib: cap_row(layer, ib))
                            for ib in range(1, NB)]
                    if layer == 0:
                        late += [((n - BK + 1) * H_APART, lambda n=n: add_h(n)) for n in range(BK, NT // 4)]
                        late += [(ib * H_APART + 3, lambda ib=ib: sum_x(ib)) for ib in range(NB)]
                    else:
                        late += items("tail", last_of_2)
                    blocks(dve, layer, adjacency_quad if layer == 0 else attention_quad,
                           at_places(layer, late + means_late), lambda ib: pieces(layer, ib))
                else:
                    late = items("mask", pieces(layer - 1, NB - 1)) + means_late
                    blocks(dve, layer, lambda ib, turn, c, late: mask_quad(layer, ib, turn, c, late),
                           at_places(layer, late), lambda ib: pieces(layer, ib))
                if layer >= 2:
                    last_of_2 = pieces(layer, NB - 1)
                    run(last_of_2, but=PLACES["tail"])

        @block.tensor
        def _(pe):
            def prepare_weights():
                pe.wait_ge(weights_in, 16 * 13)
                pe.wait_ge(fold_ready, 9)
                for n in range(3):
                    nc.tensor.matmul(epi[0][:, n * D:(n + 1) * D], fold_t[:, :], w_raw[:, n + 1, :], start=True, stop=True)
                nc.tensor.matmul(epi[1][:, 0:2], w_tr[0], a_cols[:, 0:2], start=True, stop=True)
                nc.tensor.matmul(epi[1][:, 2:4], w_tr[1], a_cols[:, 2:4], start=True, stop=True)
                nc.tensor.matmul(epi[1][:, 4:6], b3_wide, a_cols[:, 2:4], start=True, stop=True)
                nc.tensor.matmul(epi[1][:, 2 * D:3 * D], a2_wide[0], w_tr[0], start=True, stop=True)
                nc.tensor.matmul(epi[1][:, D:2 * D], a2_wide[1], w_tr[1], start=True, stop=True)\
                    .then_inc(fold_products, 1)
                pe.wait_ge(weights_ready, 1)

            def row_product(g):
                pe.wait_ge(s1_wide_ready, 1)
                if g >= BK:
                    pe.wait_ge(x_t_in[g // BK], 16)
                    pe.wait_ge(s0_used, 1)
                    pe.wait_ge(of(0, "row_exps"), g)
                    if (g - BK) * H_APART + 1 > PLACES["mean_0"]["mean"]:
                        pe.wait_ge(of(0, "mean_ready"), 1)
                b = g % BK
                nc.tensor.matmul(acc[:, b, :] if g < BK else small[:, :], s1_wide[0][:, :],
                                 x_t_sb[g // BK][:, b * BANK:(b + 1) * BANK], start=True, stop=True)\
                    .then_inc(of(0, "row_ready"), 1)

            def first_s():
                for ib in range(NB // 2):
                    pe.wait_ge(x_t_in[ib], 16)
                    if ib == 0:
                        for g in range(BK):
                            row_product(g)
                    for t in range(BT):
                        mm = nc.tensor.matmul(SNAT[:, ib * BT + t, :], x_t_sb[ib][:, t * P:(t + 1) * P], sv0[:, :],
                                              start=True, stop=True)
                mm.then_inc(s0_ready, 1)

            def h_products(n):
                if n >= EB:
                    pe.wait_ge(h_used, n - EB + 1)
                pe.wait_ge(x_t_in[n // BK], 16)
                for k in range(4):
                    t = n % BK * 4 + k
                    mm = nc.tensor.matmul(epi[n % EB][:, k * D:(k + 1) * D], x_t_sb[n // BK][:, t * P:(t + 1) * P],
                                          w_raw[:, 0, :], start=True, stop=True)
                mm.then_inc(h_ready, 1)

            def mean_pieces(layer):
                def column():
                    pe.wait_ge(of(layer, "sum_ready"), NB)
                    if layer == 3:
                        pe.wait_ge(of(3, "s1_copied"), NB * BK + BK)
                    for b in range(NB):
                        mm = nc.tensor.matmul(COL, x_part[:, b, :], ones[:, 0:1], start=(b == 0), stop=(b == NB - 1))
                    mm.then_inc(of(layer, "col_ready"), 1)

                def mean():
                    if layer == 0:
                        pe.wait_ge(of(0, "sum_ready"), NB)
                        pe.wait_ge(of(0, "row_exps"), BK + (PLACES["mean_0"]["mean"] - 1) // H_APART + 1)
                        for b in range(NB):
                            mm = nc.tensor.matmul(MEAN, ones[:, :], x_part[:, b, :], start=(b == 0), stop=(b == NB - 1))
                    else:
                        pe.wait_ge(of(layer, "col_copied"), 1)
                        mm = nc.tensor.matmul(MEAN, t_wide, w_raw[:, layer, :], start=True, stop=True)
                    mm.then_inc(of(layer, "mean_product"), 1)

                return {"column": column, "mean": mean} if layer else {"mean": mean}

            def pieces(layer, ib):
                def project(groups):
                    if groups[0] == 0:
                        pe.wait_ge(of(layer, "sums_ready"), ib * BK + 2 * BK)
                        if layer == 2:
                            pe.wait_ge(of(3, "s1_copied"), ib * BK + BK)
                    for g in groups:
                        pe.wait_ge(of(layer, "proj_read"), ib * NG + (g + 1))
                        for t in range(g * GT, min(g * GT + GT, BT)):
                            k = t - g * GT
                            mm = nc.tensor.matmul(epi[g % EB][:, k * (D + 1):(k + 1) * (D + 1)],
                                                  sums_t[:, t * P:(t + 1) * P], proj[layer][:, :], start=True, stop=True)
                        mm.then_inc(of(layer, "proj_ready"), 1)

                def turn():
                    pe.wait_ge(of(layer, "normed"), ib + 1)
                    for g in range(BK):
                        for k in range(4):
                            mm = nc.tensor.transpose(banks[g][:, k * P:(k + 1) * P], res[:, g * 4 + k, :], ident[:, :])
                        mm.then_inc(of(layer, "tr_ready"), 1)

                def s1_rows():
                    pe.wait_ge(of(layer, "tr_copied"), ib * BK + BK)
                    for g in range(BK):
                        nc.tensor.matmul(banks[g], s1_wide[3][:, :], sq[:, g * BANK:(g + 1) * BANK],
                                         start=True, stop=True).then_inc(of(3, "s1_ready"), 1)

                late = {f"project_{n + 1}": lambda n=n: project(groups_of(n)) for n in range(PROJECTIONS)}
                if layer == 2:
                    late.update(turn=turn, s1_rows=s1_rows)
                return late

            def quad(layer, ib, turn, c, late):
                q = turn * QR + c
                first, last = is_at(turn, 0) and c == 0, is_at(turn, TURNS - 1) and c == QR - 1
                if layer not in ATTENTION:
                    pe.wait_ge(of(layer, "mask_ready"), ib * NQ + q + 1)
                    if is_at(ib, 0) and c == 0:
                        pe.wait_ge(of(layer, "lo_ready"), turn + 1)
                for k in range(SLOTS):
                    step = ib * NT + q * SLOTS + k
                    start, stop = first and k == 0, last and k == SLOTS - 1
                    if layer in ATTENTION:
                        pe.wait_ge(of(layer, "prob_ready"), step + 1)
                        pe.wait_ge(of(layer, "xs_ready"), step * 2 + 2)
                    for h in range(1 if layer in ATTENTION else 2):
                        for b in range(BK):
                            if start and h == 0:
                                pe.wait_ge(of(layer, "sums_ready"), ib * BK + (b + 1))
                            if layer in ATTENTION:
                                mm = nc.tensor.matmul(acc[:, b, :], xs[:, k, :], prob[:, k, b * BANK:(b + 1) * BANK],
                                                      start=start, stop=stop)
                            else:
                                w = parts[layer][:, bass.ds(turn, 1), h, c * SLOTS + k, :].rearrange("p a d -> p (a d)")
                                mm = nc.tensor.matmul(acc[:, b, :], w, mask[:, c % MR, k, b * BANK:(b + 1) * BANK],
                                                      start=start and h == 0, stop=stop and h == 1)
                    if layer in ATTENTION:
                        mm.then_inc(of(layer, "prob_used"), 1)
                    elif k == SLOTS - 1:
                        mm.then_inc(quad_used, 1)
                    if layer in ATTENTION:
                        late[k]()
                    elif k % 2:
                        late[k // 2]()

            prepare_weights()
            first_s()
            for n in range(BK):
                h_products(n)
            for layer in LAYERS:
                if layer in ATTENTION:
                    pe.sem_inc(of(layer, "prob_used"), SLOTS)
                elif layer == 1:
                    pe.sem_inc(quad_used, MR)
                if layer:
                    pe.wait_ge(of(layer - 1, "sums_ready"), NB * BK + BK)
                pe.sem_inc(of(layer, "proj_read"), EB)
                pe.sem_inc(of(layer, "sums_ready"), BK)
                if layer == 2:
                    pe.sem_inc(of(3, "s1_copied"), BK)
                means_late = items(f"mean_{layer}", mean_pieces(layer)) if layer in MEAN_ROWS else []
                if layer == 0:
                    pe.wait_ge(of(0, "row_exps"), BK)
                    late = [((g - BK) * H_APART + 1, lambda g=g: (h_products(g), row_product(g)))
                            for g in range(BK, NB * BK)]
                elif layer < 3:
                    late = items("mask", pieces(layer - 1, NB - 1))
                else:
                    late = items("tail", last_of_2)
                blocks(pe, layer, lambda ib, turn, c, late: quad(layer, ib, turn, c, late),
                       at_places(layer, late + means_late), lambda ib: pieces(layer, ib), peel_last=True)
                if layer >= 2:
                    last_of_2 = pieces(layer, NB - 1)
                    run(last_of_2, but=PLACES["tail"])


_LAYOUT = {
    "x": lambda i: i["x"],
    "x_t": lambda i: i["x"].T,
    "adj": lambda i: i["adj"].T.reshape(i["adj"].shape[1] // P, P, i["adj"].shape[0] // BW, BW)
    .transpose(2, 0, 1, 3).reshape(-1, P, BW),
    "w0": lambda i: i["L0_gnn_W"], "w0_t": lambda i: i["L0_gnn_W"].T,
    "a0": lambda i: i["L0_gnn_a"].reshape(2, -1).T,
    "w1": lambda i: i["L1_gnn_W"], "gamma": lambda i: i["L1_gnn_gamma"], "beta": lambda i: i["L1_gnn_beta"],
    "w2_t": lambda i: i["L2_gnn_W"].T, "b2": lambda i: i["L2_gnn_b"],
    "w3": lambda i: i["L3_gnn_W_w"], "w3_t": lambda i: i["L3_gnn_W_w"].T,
    "a3": lambda i: i["L3_gnn_a"].reshape(2, -1).T, "b3": lambda i: i["L3_gnn_W_b"],
}


def kernel(**inputs):
    import numpy as _np
    import concourse.bacc as _bacc
    from concourse import mybir as _mybir
    from concourse.bass_utils import run_bass_kernel_spmd as _run

    nc = _bacc.Bacc("TRN2", target_bir_lowering=False, num_devices=1)
    inputs = {name: _np.asarray(a) for name, a in inputs.items()}
    arrays, args = {}, []
    for name, lay in _LAYOUT.items():
        a = _np.ascontiguousarray(lay(inputs))
        arrays[f"in_{name}"] = a
        args.append(nc.dram_tensor(f"in_{name}", a.shape, _mybir.dt.from_np(a.dtype), kind="ExternalInput").ap())
    out = nc.dram_tensor("out_0", inputs["x"].shape, _mybir.dt.float32, kind="ExternalOutput").ap()
    graph_layers(nc, *args, out)
    r = _run(nc, [arrays], core_ids=[0])
    return r.results[0]["out_0"]
```
